# Optimizing a Trainium2 kernel written in Bass

```python
import numpy as np
import jax
import jax.numpy as jnp

def _softmax(x, axis=-1):
    return jax.nn.softmax(x, axis=axis)

def _gelu(x):
    return jax.nn.gelu(x, approximate=True)

def _silu(x):
    return jax.nn.silu(x)

def _sigmoid(x):
    return jax.nn.sigmoid(x)

def _layernorm(x, axis=-1, eps=1e-05):
    m = jnp.mean(x, axis=axis, keepdims=True)
    v = jnp.var(x, axis=axis, keepdims=True)
    return (x - m) / jnp.sqrt(v + eps)

def _scatter_add(tgt, idx, src, axis=0):
    return tgt.at[idx].add(src)

def _segment_sum(src, seg, n):
    return jax.ops.segment_sum(src, seg, n)
kernel_name = 'mk_flamingo_gated_d2_seqx_r8_d3dcd9'

def setup_inputs(seed: int=0):
    np.random.seed(seed)
    _w = jnp.asarray

    def _rec_inputs():
        import jax
        import jax.numpy as jnp
        _rk = jax.random.key(seed)
        x = 7.22e-05 + 1 * jax.random.normal(jax.random.fold_in(_rk, 1), (16, 64, 128), jnp.float32)
        _lenS = 64 - jax.random.randint(jax.random.fold_in(_rk, 7), (16,), 0, max(1, 64 // 4) + 1, jnp.int32)
        _lenS2 = 64 - jax.random.randint(jax.random.fold_in(_rk, 8), (16,), 0, max(1, 64 // 4) + 1, jnp.int32)
        _ctx_1024P = jax.random.normal(jax.random.fold_in(_rk, 11), (16, 16, 128), jnp.float32)
        _ctx_1024c = jax.random.dirichlet(jax.random.fold_in(_rk, 511), 0.3 * jnp.ones((16,), jnp.float32), (16, 64))
        _ctx_1024t = jnp.einsum('bsk,bkd->bsd', _ctx_1024c, _ctx_1024P)
        _ctx_1024t = _ctx_1024t * jax.lax.rsqrt(jnp.mean(jnp.square(_ctx_1024t)) + 1e-12) * 0.953939
        ctx_1024 = 4.13588e-05 + 0.999923 * (_ctx_1024t + 0.3 * jax.random.normal(jax.random.fold_in(_rk, 611), (16, 64, 128), jnp.float32))
        _g = jax.random.normal(jax.random.fold_in(_rk, 9001), (2, 2), jnp.float32)
        _g = jnp.sign(_g) * jnp.maximum(jnp.abs(_g), 1.0) + (_g == 0) * 1.0
        g_xattn = _g[0]
        g_ffn = _g[1]
        return (x, ctx_1024, g_xattn, g_ffn)
    x, ctx_1024, g_xattn, g_ffn = _rec_inputs()

    def _L0_xattn_setup():
        import jax, jax.numpy as jnp
        import numpy as np
        D_EMB = 128
        N_HEADS = 16
        D_K = D_EMB // N_HEADS
        B, L = (4, 256)
        key = jax.random.key(seed)
        kx, kc, kq, kk, kv, ko = jax.random.split(key, 6)
        bound = float(np.sqrt(3.0 / D_EMB))
        uni = lambda k: jax.random.uniform(k, (D_EMB, D_EMB), jnp.float32, -bound, bound)
        return {'x': jax.random.normal(kx, (B, L, D_EMB), jnp.float32), 'context': jax.random.normal(kc, (B, L, D_EMB), jnp.float32), 'Wq': uni(kq), 'Wk': uni(kk), 'Wv': uni(kv), 'Wo': uni(ko)}
    _L0_xattn_all = _L0_xattn_setup()
    _L0_xattn_in = {k: v for k, v in _L0_xattn_all.items() if k in ('Wq', 'Wk', 'Wv', 'Wo')}
    del _L0_xattn_all

    def _L0_ffn_setup():
        import jax, jax.numpy as jnp
        import numpy as np
        from jax import lax
        TOP_K = 4
        N_GROUP = 4
        TOPK_GROUP = 2
        ROUTED_SCALE = 2.5
        NEG_INF = -1000000000.0

        def _route(xf, router_weight, router_bias):
            T = xf.shape[0]
            E = router_weight.shape[0]
            logits = xf @ router_weight.T
            scores = jax.nn.sigmoid(logits)
            s_choice = scores + router_bias
            per_group = E // N_GROUP
            sg = s_choice.reshape(T, N_GROUP, per_group)
            group_scores = lax.top_k(sg, 2)[0].sum(-1)
            _, gidx = lax.top_k(group_scores, TOPK_GROUP)
            gmask = jnp.zeros((T, N_GROUP), dtype=bool).at[jnp.arange(T)[:, None], gidx].set(True)
            masked = jnp.where(gmask[:, :, None], sg, NEG_INF).reshape(T, E)
            _, topk_idx = lax.top_k(masked, TOP_K)
            w = jnp.take_along_axis(scores, topk_idx, axis=1)
            w = w / (w.sum(-1, keepdims=True) + 1e-20) * ROUTED_SCALE
            combine = jnp.zeros((T, E), dtype=xf.dtype).at[jnp.arange(T)[:, None], topk_idx].add(w)
            return combine
        key = jax.random.key(seed)
        ks = jax.random.split(key, 6)
        B, S, H, I, E = (2, 256, 128, 64, 16)
        x = jax.random.normal(ks[0], (B, S, H), dtype=jnp.float32)
        router_weight = jax.random.normal(ks[1], (E, H), dtype=jnp.float32) * 0.02
        router_bias = jnp.zeros((E,), dtype=jnp.float32)
        w_gate = jax.random.normal(ks[2], (E, I, H), dtype=jnp.float32) * 0.02
        w_up = jax.random.normal(ks[3], (E, I, H), dtype=jnp.float32) * 0.02
        w_down = jax.random.normal(ks[4], (E, H, I), dtype=jnp.float32) * 0.02
        return {'x': x, 'router_weight': router_weight, 'router_bias': router_bias, 'w_gate': w_gate, 'w_up': w_up, 'w_down': w_down}
    _L0_ffn_all = _L0_ffn_setup()
    _L0_ffn_in = {k: v for k, v in _L0_ffn_all.items() if k in ('router_weight', 'router_bias', 'w_gate', 'w_up', 'w_down')}
    del _L0_ffn_all

    def _L1_xattn_setup():
        import jax, jax.numpy as jnp
        import numpy as np
        key = jax.random.key(seed)
        k1, k2, k3 = jax.random.split(key, 3)
        B, L, D = (8, 256, 128)
        ix = jax.random.normal(k1, (B, L, D), dtype=jnp.float32)
        iother = jax.random.normal(k2, (B, L, D), dtype=jnp.float32)
        W = jax.random.normal(k3, (D, D), dtype=jnp.float32) * (1.0 / np.sqrt(D))
        b = jnp.zeros((D,), dtype=jnp.float32)
        return {'ix': ix, 'iother': iother, 'W': W, 'b': b}
    _L1_xattn_all = _L1_xattn_setup()
    _L1_xattn_in = {k: v for k, v in _L1_xattn_all.items() if k in ('W', 'b')}
    del _L1_xattn_all

    def _L1_ffn_setup():
        import jax, jax.numpy as jnp
        import numpy as np
        D_MODEL, D_FF, RANK = (128, 512, 32)
        B, S = (4, 512)
        key = jax.random.key(seed)
        ks = jax.random.split(key, 7)
        return {'x': jax.random.normal(ks[0], (B, S, D_MODEL), dtype=jnp.float32), 'U1': jax.random.normal(ks[1], (D_MODEL, RANK), dtype=jnp.float32) * 0.02, 'V1': jax.random.normal(ks[2], (RANK, D_FF), dtype=jnp.float32) * 0.02, 'b1': jnp.zeros((D_FF,), dtype=jnp.float32), 'U2': jax.random.normal(ks[3], (D_FF, RANK), dtype=jnp.float32) * 0.02, 'V2': jax.random.normal(ks[4], (RANK, D_MODEL), dtype=jnp.float32) * 0.02, 'b2': jnp.zeros((D_MODEL,), dtype=jnp.float32)}
    _L1_ffn_all = _L1_ffn_setup()
    _L1_ffn_in = {k: v for k, v in _L1_ffn_all.items() if k in ('U1', 'V1', 'b1', 'U2', 'V2', 'b2')}
    del _L1_ffn_all
    return {'x': x, 'ctx_1024': ctx_1024, 'g_xattn': g_xattn, 'g_ffn': g_ffn, 'L0_xattn_Wq': _L0_xattn_in['Wq'], 'L0_xattn_Wk': _L0_xattn_in['Wk'], 'L0_xattn_Wv': _L0_xattn_in['Wv'], 'L0_xattn_Wo': _L0_xattn_in['Wo'], 'L0_ffn_router_weight': _L0_ffn_in['router_weight'], 'L0_ffn_router_bias': _L0_ffn_in['router_bias'], 'L0_ffn_w_gate': _L0_ffn_in['w_gate'], 'L0_ffn_w_up': _L0_ffn_in['w_up'], 'L0_ffn_w_down': _L0_ffn_in['w_down'], 'L1_xattn_W': _L1_xattn_in['W'], 'L1_xattn_b': _L1_xattn_in['b'], 'L1_ffn_U1': _L1_ffn_in['U1'], 'L1_ffn_V1': _L1_ffn_in['V1'], 'L1_ffn_b1': _L1_ffn_in['b1'], 'L1_ffn_U2': _L1_ffn_in['U2'], 'L1_ffn_V2': _L1_ffn_in['V2'], 'L1_ffn_b2': _L1_ffn_in['b2']}

def reference(x, ctx_1024, g_xattn, g_ffn, L0_xattn_Wq, L0_xattn_Wk, L0_xattn_Wv, L0_xattn_Wo, L0_ffn_router_weight, L0_ffn_router_bias, L0_ffn_w_gate, L0_ffn_w_up, L0_ffn_w_down, L1_xattn_W, L1_xattn_b, L1_ffn_U1, L1_ffn_V1, L1_ffn_b1, L1_ffn_U2, L1_ffn_V2, L1_ffn_b2):
    import jax
    import jax.numpy as jnp

    def _L0_xattn_ref(x, context, Wq, Wk, Wv, Wo):
        import jax, jax.numpy as jnp
        import numpy as np
        D_EMB = 128
        N_HEADS = 16
        D_K = D_EMB // N_HEADS
        B, L = (4, 256)
        b, length, d = x.shape
        Q = (x @ Wq.T).reshape(b, length, N_HEADS, D_K).swapaxes(-2, -1)
        K = (context @ Wk.T).reshape(b, length, N_HEADS, D_K).swapaxes(-2, -1)
        V = (context @ Wv.T).reshape(b, length, N_HEADS, D_K).swapaxes(-2, -1)
        qk = jnp.einsum('blih,bljh->blij', Q, K) / jnp.sqrt(jnp.asarray(D_K, x.dtype))
        attn = jax.nn.softmax(qk, axis=-1)
        valued = jnp.einsum('blij,bljh->blih', attn, V)
        concat = valued.swapaxes(-2, -1).reshape(b, length, d)
        return concat @ Wo.T

    def _L0_ffn_ref(x, router_weight, router_bias, w_gate, w_up, w_down):
        import jax, jax.numpy as jnp
        import numpy as np
        from jax import lax
        TOP_K = 4
        N_GROUP = 4
        TOPK_GROUP = 2
        ROUTED_SCALE = 2.5
        NEG_INF = -1000000000.0

        def _route(xf, router_weight, router_bias):
            T = xf.shape[0]
            E = router_weight.shape[0]
            logits = xf @ router_weight.T
            scores = jax.nn.sigmoid(logits)
            s_choice = scores + router_bias
            per_group = E // N_GROUP
            sg = s_choice.reshape(T, N_GROUP, per_group)
            group_scores = lax.top_k(sg, 2)[0].sum(-1)
            _, gidx = lax.top_k(group_scores, TOPK_GROUP)
            gmask = jnp.zeros((T, N_GROUP), dtype=bool).at[jnp.arange(T)[:, None], gidx].set(True)
            masked = jnp.where(gmask[:, :, None], sg, NEG_INF).reshape(T, E)
            _, topk_idx = lax.top_k(masked, TOP_K)
            w = jnp.take_along_axis(scores, topk_idx, axis=1)
            w = w / (w.sum(-1, keepdims=True) + 1e-20) * ROUTED_SCALE
            combine = jnp.zeros((T, E), dtype=xf.dtype).at[jnp.arange(T)[:, None], topk_idx].add(w)
            return combine
        B, S, H = x.shape
        E = w_gate.shape[0]
        xf = x.reshape(-1, H)
        combine = _route(xf, router_weight, router_bias)
        out = jnp.zeros_like(xf)
        for e in range(E):
            g = xf @ w_gate[e].T
            u = xf @ w_up[e].T
            y_e = jax.nn.silu(g) * u @ w_down[e].T
            out = out + combine[:, e:e + 1] * y_e
        return out.reshape(B, S, H)

    def _L1_xattn_ref(ix, iother, W, b):
        import jax, jax.numpy as jnp
        import numpy as np
        ex = ix @ W.T + b
        eother = iother @ W.T + b
        align = jnp.einsum('bld,bmd->blm', ex, eother)
        align = jax.nn.softmax(align, axis=-1)
        aligned = jnp.einsum('blm,bmd->bld', align, iother)
        return aligned

    def _L1_ffn_ref(x, U1, V1, b1, U2, V2, b2):
        import jax, jax.numpy as jnp
        import numpy as np
        D_MODEL, D_FF, RANK = (128, 512, 32)
        B, S = (4, 512)
        P = jnp.einsum('bsd,dr->bsr', x, U1)
        H = jax.nn.gelu(jnp.einsum('bsr,rf->bsf', P, V1) + b1)
        Q = jnp.einsum('bsf,fr->bsr', H, U2)
        return jnp.einsum('bsr,rd->bsd', Q, V2) + b2
    x = x + jnp.tanh(g_xattn[0]) * _L0_xattn_ref(_layernorm(x, axis=-1), ctx_1024, L0_xattn_Wq, L0_xattn_Wk, L0_xattn_Wv, L0_xattn_Wo)
    x = x + jnp.tanh(g_ffn[0]) * _L0_ffn_ref(_layernorm(x, axis=-1), L0_ffn_router_weight, L0_ffn_router_bias, L0_ffn_w_gate, L0_ffn_w_up, L0_ffn_w_down)
    x = x + jnp.tanh(g_xattn[1]) * _L1_xattn_ref(_layernorm(x, axis=-1), ctx_1024, L1_xattn_W, L1_xattn_b)
    x = x + jnp.tanh(g_ffn[1]) * _L1_ffn_ref(_layernorm(x, axis=-1), L1_ffn_U1, L1_ffn_V1, L1_ffn_b1, L1_ffn_U2, L1_ffn_V2, L1_ffn_b2)
    return x

_drawn_inputs = setup_inputs


def setup_inputs(seed=0):
    import zlib

    import numpy as np

    out = dict(_drawn_inputs(seed))
    spreads = {'g_ffn': (-1.0, 0.6),
     'L0_ffn_router_bias': (0.0, 0.8),
     'L1_xattn_b': (0.0, 0.1),
     'L1_ffn_b1': (0.0, 0.8),
     'L1_ffn_b2': (0.0, 0.382)}
    factors = {'L0_ffn_router_weight': 8.0,
     'L0_ffn_w_gate': 7.044,
     'L0_ffn_w_up': 7.748,
     'L0_ffn_w_down': 8.0,
     'L1_ffn_U1': 8.0,
     'L1_ffn_V1': 8.0,
     'L1_ffn_U2': 8.0,
     'L1_ffn_V2': 8.0}
    for name, (base, spread) in spreads.items():
        noise = np.random.default_rng([zlib.crc32(name.encode()), seed]).standard_normal(out[name].shape)
        drawn = base * np.exp(spread * noise) if base else spread * noise
        out[name] = jnp.asarray(drawn.astype(out[name].dtype))
    for name, factor in factors.items():
        out[name] = (out[name] * factor).astype(out[name].dtype)
    return out
```

```python
from contextlib import ExitStack

import numpy as np

import concourse.bass as bass
from concourse import mybir

F32 = mybir.dt.float32
BF16 = mybir.dt.bfloat16
ALU = mybir.AluOpType
ACT = mybir.ActivationFunctionType
AX = mybir.AxisListType

P = 128
D = 128
TOKENS = 1024
TILES = 2
CT = TILES * P
CHUNKS = TOKENS // CT
SEQ = 64
HEADS, DK = 16, 8
PAIRS_IJ = DK * DK
EXPERTS, INNER = 16, 64
GROUPS = 4
PER_GROUP = EXPERTS // GROUPS
TOP_K, TOP_GROUPS = 4, 2
EXPERT_PAIRS = EXPERTS // 2
STEPS = EXPERT_PAIRS // 2
ROUTED_SCALE = 2.5
EPS = 1e-5
MASKED, TAKEN = -1e9, -3e9
PARTS = 3
FF, RANK = 512, 32
FF_CHUNKS = FF // P

_EARLY = [("ident", P), ("wq", D), ("wkv", 2 * D), ("wo", D), ("router", EXPERTS)]
_LATE = [("wx", D), ("u1", RANK), ("u2", FF_CHUNKS * RANK), ("v2", D), ("bx", 1), ("b1", FF_CHUNKS)]


def columns(parts):
    at, out = 0, {}
    for name, n in parts:
        out[name] = (at, at + n)
        at += n
    return out, at


EARLY, EARLY_COLS = columns(_EARLY)
LATE, LATE_COLS = columns(_LATE)


def program(nc, x, ctx_t, ctx_m, gates, early, late, experts_in, experts_out, v1, router_bias, b2,
            earlier, select, ident_bf, out):
    with ExitStack() as ctx:
        def sb(name, shape, dt=F32):
            return ctx.enter_context(nc.sbuf_tensor(name, shape, dt))

        def bank(name):
            return ctx.enter_context(nc.psum_tensor(name, [P, 512], F32))

        def sem(name):
            return ctx.enter_context(nc.semaphore(name))

        psA0, psA1 = bank("psA0"), bank("psA1")
        psG, psU, psC, psY = bank("psG"), bank("psU"), bank("psC"), bank("psY")
        psL0, psL1 = bank("psL0"), bank("psL1")

        w_early = sb("w_early", [P, EARLY_COLS])
        w_late = sb("w_late", [P, LATE_COLS])
        w_gate = sb("w_gate", [P, EXPERTS * INNER])
        w_up = sb("w_up", [P, EXPERTS * INNER])
        w_down = sb("w_down", [P, EXPERT_PAIRS, D])
        w_v1 = sb("w_v1", [RANK, FF])
        bias_r = sb("bias_r", [P, EXPERTS])
        b2_rows = sb("b2_rows", [P, D])
        earlier_s = sb("earlier_s", [P, GROUPS, GROUPS], mybir.dt.int32)
        select_s = sb("select_s", [PARTS * EXPERTS, EXPERT_PAIRS, P], BF16)
        identb = sb("identb", [P, P], BF16)
        gates_s = sb("gates_s", [P, 4])
        tg = sb("tg", [P, 4])
        tg_moe = sb("tg_moe", [P, 1])
        b2g = sb("b2g", [P, D])
        neg_half = sb("neg_half", [P, TILES])

        def E(name):
            a, b = EARLY[name]
            return w_early[:, a:b]

        def L(name):
            a, b = LATE[name]
            return w_late[:, a:b]

        X = sb("X", [P, CHUNKS * TILES, D])
        ctxT = sb("ctxT", [P, TOKENS])
        ctxM = sb("ctxM", [SEQ, TOKENS // SEQ, D])

        def norm_buffers(n):
            return dict(
                st=sb(f"st{n}", [P, TILES, 6]), mv=sb(f"mv{n}", [P, TILES, 2]),
                ve=sb(f"ve{n}", [P, TILES]), rstd=sb(f"rstd{n}", [P, TILES]),
                xn=sb(f"xn{n}", [P, CT]), xnT=sb(f"xnT{n}", [P, CT]))

        NORM = {n: norm_buffers(n) for n in "ABCD"}
        qkv = sb("qkv", [P, TILES, 3 * D])
        prod = sb("prod", [P, TILES, HEADS * PAIRS_IJ])
        score = sb("score", [P, TILES, PAIRS_IJ])
        smax = sb("smax", [P, TILES * DK])
        shifted = sb("shifted", [P, TILES * PAIRS_IJ])
        expd = sb("expd", [P, TILES * PAIRS_IJ])
        esum = sb("esum", [P, TILES * DK])
        erec = sb("erec", [P, TILES * DK])
        attn = sb("attn", [P, TILES, PAIRS_IJ])
        prod2 = sb("prod2", [P, TILES, HEADS * PAIRS_IJ])
        val = sb("val", [P, TILES, D])
        valT = sb("valT", [P, CT])

        TE, TG = TILES * EXPERTS, TILES * GROUPS
        r_exp, r_den, r_score, r_choice = (sb(n, [P, TE]) for n in ("r_exp", "r_den", "r_score", "r_choice"))
        r_hi, r_lo = sb("r_hi", [P, TG, 2]), sb("r_lo", [P, TG, 2])
        r_m1, r_mm, r_ml, r_m2, r_gs = (sb(n, [P, TG]) for n in ("r_m1", "r_mm", "r_ml", "r_m2", "r_gs"))
        r_ge, r_gt = sb("r_ge", [P, TILES, GROUPS * GROUPS]), sb("r_gt", [P, TILES, GROUPS * GROUPS])
        r_rank, r_keep, r_pen = sb("r_rank", [P, TG]), sb("r_keep", [P, TG]), sb("r_pen", [P, TG])
        r_kept, r_masked = sb("r_kept", [P, TE]), sb("r_masked", [P, TE])
        r_top = sb("r_top", [P, TILES, 8])
        r_marked, r_chosen, r_weight = sb("r_marked", [P, TE]), sb("r_chosen", [P, TE]), sb("r_weight", [P, TE])
        r_sum, r_sume, r_rec = (sb(n, [P, TILES]) for n in ("r_sum", "r_sume", "r_rec"))
        r_comb, r_rest, r_rest2 = sb("r_comb", [P, TE]), sb("r_rest", [P, TE]), sb("r_rest2", [P, TE])
        r_parts = sb("r_parts", [P, TILES, PARTS, EXPERTS], BF16)
        combT = sb("combT", [PARTS * EXPERTS, CT], BF16)
        gated = sb("gated", [P, 2, 2 * CT])
        weighted = sb("weighted", [P, 2 * CT])
        hid = sb("hid", [P, 2, 2 * CT])

        eT = sb("eT", [P, 2 * CT])
        nmax = sb("nmax", [P, TILES])
        psum_e = sb("psum_e", [P, TILES])
        probs = sb("probs", [P, TILES, SEQ])
        prec = sb("prec", [P, TILES])
        pgate = sb("pgate", [P, TILES])
        probsT = sb("probsT", [SEQ, CT])

        xb = sb("xb", [P, CT])
        rankT = sb("rankT", [RANK, CT])
        ff = sb("ff", [P, FF_CHUNKS, CT])
        qT = sb("qT", [P, CT])

        s_x = [sem(f"s_xin{c}") for c in range(CHUNKS)]
        s_early, s_ctxT, s_ctxM, s_gates = sem("s_early"), sem("s_ctxT"), sem("s_ctxM"), sem("s_gates")
        s_smallB, s_wgate, s_wup, s_wdown, s_late = (
            sem("s_smallB"), sem("s_wgate"), sem("s_wup"), sem("s_wdown"), sem("s_late"))
        s_out = sem("s_out")
        s_tanh, s_b2g, s_half = sem("s_tanh"), sem("s_b2g"), sem("s_half")
        s_dve = sem("s_dve")
        s_pool = sem("s_pool")
        s_stats = {n: sem(f"s_stats{n}") for n in "ABCD"}
        s_rstd = {n: sem(f"s_rstd{n}") for n in "ABCD"}
        s_xn = {n: sem(f"s_xn{n}") for n in "ABCD"}
        s_xnP = {n: sem(f"s_xnP{n}") for n in "ABCD"}
        s_xnT = {n: sem(f"s_xnT{n}") for n in "ABCD"}
        s_qkvP, s_qkv = sem("s_qkvP"), sem("s_qkv")
        s_prod, s_sub, s_exp, s_attn, s_prod2, s_val = (
            sem("s_prod"), sem("s_sub"), sem("s_exp"), sem("s_attn"), sem("s_prod2"), sem("s_val"))
        s_valP, s_valT, s_woP, s_x1 = sem("s_valP"), sem("s_valT"), sem("s_woP"), sem("s_x1")
        s_logit, s_rexp, s_parts, s_combP, s_combT = (
            sem("s_logit"), sem("s_rexp"), sem("s_parts"), sem("s_combP"), sem("s_combT"))
        s_gP, s_uP, s_cP, s_silu, s_weighted, s_hid, s_down = (
            sem("s_gP"), sem("s_uP"), sem("s_cP"), sem("s_silu"), sem("s_weighted"), sem("s_hid"), sem("s_down"))
        s_x2 = sem("s_x2")
        s_eP, s_eT, s_align, s_nmax, s_probs, s_probsP, s_probsT, s_avP, s_x3 = (
            sem("s_eP"), sem("s_eT"), sem("s_align"), sem("s_nmax"), sem("s_probs"), sem("s_probsP"),
            sem("s_probsT"), sem("s_avP"), sem("s_x3"))
        s_rankP, s_rankT, s_ffP, s_ff, s_qP, s_qT, s_ffoutP, s_xb, s_x4 = (
            sem("s_rankP"), sem("s_rankT"), sem("s_ffP"), sem("s_ff"), sem("s_qP"), sem("s_qT"),
            sem("s_ffoutP"), sem("s_xb"), sem("s_x4"))

        block = ctx.enter_context(nc.Block())

        def rows(c):
            return X[:, TILES * c:TILES * (c + 1), :].rearrange("p t d -> p (t d)")

        combP = psY[0:PARTS * EXPERTS, 0:CT // 2].bitcast(BF16)

        def score_product(engine, t):
            q = qkv[:, t, 0:D].rearrange("p (h i) -> p i h", h=HEADS).unsqueeze(2)
            k = qkv[:, t, D:2 * D].rearrange("p (h j) -> p j h", h=HEADS).unsqueeze(1)
            shape = [P, DK, DK, HEADS]
            return engine.tensor_tensor(prod[:, t, :].rearrange("p (i j h) -> p i j h", i=DK, j=DK),
                                        q.to_broadcast(shape), k.to_broadcast(shape), ALU.mult)

        def value_product(engine, t):
            a = attn[:, t, :].rearrange("p (i j) -> p i j", i=DK).unsqueeze(1)
            v = qkv[:, t, 2 * D:3 * D].rearrange("p (h j) -> p h j", h=HEADS).unsqueeze(2)
            shape = [P, HEADS, DK, DK]
            return engine.tensor_tensor(prod2[:, t, :].rearrange("p (h i j) -> p h i j", h=HEADS, i=DK),
                                        a.to_broadcast(shape), v.to_broadcast(shape), ALU.mult)

        @block.sync
        def _(sp):
            xv = x.rearrange("(n p) d -> p n d", p=P)
            sp.dma_start(X[:, 0:TILES, :], xv[:, 0:TILES, :]).then_inc(s_x[0], 16)
            sp.dma_start(w_early[:], early).then_inc(s_early, 16)
            sp.dma_start(ctxT[:], ctx_t).then_inc(s_ctxT, 16)
            for c in range(1, CHUNKS):
                sp.dma_start(X[:, TILES * c:TILES * (c + 1), :],
                             xv[:, TILES * c:TILES * (c + 1), :]).then_inc(s_x[c], 16)
            sp.dma_start(bias_r[:], router_bias.partition_broadcast(P)).then_inc(s_smallB, 16)
            sp.dma_start(earlier_s[:], earlier).then_inc(s_smallB, 16)
            sp.dma_start(select_s[:], select).then_inc(s_smallB, 16)
            sp.dma_start(identb[:], ident_bf).then_inc(s_smallB, 16)
            sp.dma_start(w_gate[:], experts_in[:, 0, :]).then_inc(s_wgate, 16)
            sp.dma_start(w_up[:], experts_in[:, 1, :]).then_inc(s_wup, 16)
            sp.dma_start(w_down[:], experts_out.rearrange("(n p) d -> p n d", p=P)).then_inc(s_wdown, 16)
            sp.dma_start(w_late[:], late).then_inc(s_late, 16)
            sp.dma_start(w_v1[:], v1).then_inc(s_late, 16)
            sp.dma_start(ctxM[:], ctx_m).then_inc(s_ctxM, 16)
            ov = out.rearrange("(n p) d -> p n d", p=P)
            for c in range(CHUNKS):
                sp.wait_ge(s_x4, c + 1)
                sp.dma_start(ov[:, TILES * c:TILES * (c + 1), :],
                             X[:, TILES * c:TILES * (c + 1), :]).then_inc(s_out, 16)
            sp.wait_ge(s_out, 16 * CHUNKS)

        @block.gpsimd
        def _(pool):
            chain = [0]

            def link(ins):
                chain[0] += 1
                ins.then_inc(s_pool, 1)
                pool.wait_ge(s_pool, chain[0])

            link(nc.gpsimd.memset(neg_half[:], -0.5))
            pool.wait_ge(s_gates, 48)
            pool.wait_ge(s_tanh, 1)
            nc.gpsimd.tensor_scalar(b2g[:], b2_rows[:], tg[:, 3:4], None, ALU.mult).then_inc(s_b2g, 1)

            def rstd(n, c):
                b = NORM[n]
                pool.wait_ge(s_stats[n], c + 1)
                link(nc.gpsimd.tensor_scalar(b["ve"][:], b["mv"][:, :, 1], EPS, None, ALU.add))
                nc.gpsimd.tensor_tensor(b["rstd"][:], b["ve"][:], neg_half[:], ALU.pow).then_inc(s_rstd[n], 1)

            def attn_product(c):
                pool.wait_ge(s_qkv, TILES * c + 2)
                score_product(nc.gpsimd, 1).then_inc(s_prod, 1)

            def value_product_pool(c):
                pool.wait_ge(s_attn, c + 1)
                value_product(nc.gpsimd, 1).then_inc(s_prod2, 1)

            def add_b2(c):
                pool.wait_ge(s_x3, c + 1)
                if c >= 1:
                    pool.wait_ge(s_x4, c)
                if c == 0:
                    pool.wait_ge(s_b2g, 1)
                nc.gpsimd.tensor_tensor(xb[:].rearrange("p (t d) -> p t d", t=TILES),
                                        X[:, TILES * c:TILES * (c + 1), :],
                                        b2g[:].unsqueeze(1).to_broadcast([P, TILES, D]), ALU.add).then_inc(s_xb, 1)

            for slot in range(CHUNKS + 2):
                a, b, l = slot, slot - 1, slot - 2
                if 0 <= b < CHUNKS:
                    rstd("B", b)
                if 0 <= l < CHUNKS:
                    rstd("C", l)
                if a < CHUNKS:
                    rstd("A", a)
                    attn_product(a)
                if 0 <= l < CHUNKS:
                    add_b2(l)
                    rstd("D", l)
                if a < CHUNKS:
                    value_product_pool(a)

        @block.vector
        def _(dve):
            V = nc.vector
            chain = [0]

            def link(ins):
                chain[0] += 1
                ins.then_inc(s_dve, 1)
                dve.wait_ge(s_dve, chain[0])

            def after():
                chain[0] += 1
                return chain[0]

            def norm_stats(n, c):
                b = NORM[n]
                for t in range(TILES):
                    V.bn_stats(b["st"][:, t, :], X[:, TILES * c + t, :]).then_inc(s_dve, 1)
                    after()
                dve.wait_ge(s_dve, chain[0])
                for t in range(TILES):
                    ins = V.bn_aggr(b["mv"][:, t, :], b["st"][:, t, :])
                ins.then_inc(s_stats[n], 1)

            def norm_apply(n, c):
                b = NORM[n]
                dve.wait_ge(s_rstd[n], c + 1)
                dve.wait_ge(s_stats[n], c + 1)
                if c >= 1:
                    dve.wait_ge(s_xnP[n], c)
                for t in range(TILES):
                    ins = V.tensor_scalar(b["xn"][:, t * D:(t + 1) * D], X[:, TILES * c + t, :],
                                          b["mv"][:, t, 0:1], b["rstd"][:, t:t + 1], ALU.subtract, ALU.mult)
                ins.then_inc(s_xn[n], 1)

            def a_scores(c):
                dve.wait_ge(s_qkv, TILES * c + 1)
                link(score_product(V, 0))
                V.tensor_reduce(score[:, 0, :], prod[:, 0, :].rearrange("p (a h) -> p a h", h=HEADS),
                                AX.X, ALU.add).then_inc(s_dve, 1)
                after()

            def a_scores1(c):
                dve.wait_ge(s_prod, c + 1)
                link(V.tensor_reduce(score[:, 1, :], prod[:, 1, :].rearrange("p (a h) -> p a h", h=HEADS),
                                     AX.X, ALU.add))

            def a_softmax_shift(c):
                sc = score[:].rearrange("p t (i j) -> p (t i) j", i=DK)
                link(V.tensor_reduce(smax[:], sc, AX.X, ALU.max))
                if c >= 1:
                    dve.wait_ge(s_exp, c)
                V.tensor_tensor(shifted[:].rearrange("p (a j) -> p a j", j=DK), sc,
                                smax[:].unsqueeze(2).to_broadcast([P, TILES * DK, DK]), ALU.subtract).then_inc(s_sub, 1)

            def a_softmax_norm(c):
                dve.wait_ge(s_exp, c + 1)
                ex = expd[:].rearrange("p (a j) -> p a j", j=DK)
                link(V.tensor_reduce(esum[:], ex, AX.X, ALU.add))
                link(V.reciprocal(erec[:], esum[:]))
                V.tensor_tensor(attn[:].rearrange("p t (i j) -> p (t i) j", i=DK), ex,
                                erec[:].unsqueeze(2).to_broadcast([P, TILES * DK, DK]), ALU.mult).then_inc(s_attn, 1)

            def a_value(c):
                dve.wait_ge(s_attn, c + 1)
                link(value_product(V, 0))
                if c >= 1:
                    dve.wait_ge(s_valP, TILES * c)
                V.tensor_reduce(val[:, 0, :], prod2[:, 0, :].rearrange("p (a j) -> p a j", j=DK),
                                AX.X, ALU.add).then_inc(s_val, 1)

            def a_value1(c):
                dve.wait_ge(s_prod2, c + 1)
                V.tensor_reduce(val[:, 1, :], prod2[:, 1, :].rearrange("p (a j) -> p a j", j=DK),
                                AX.X, ALU.add).then_inc(s_val, 1)

            def a_out(c):
                dve.wait_ge(s_woP, c + 1)
                V.scalar_tensor_tensor(rows(c), psA1[:, 0:CT], tg[:, 0:1], rows(c), ALU.mult, ALU.add).then_inc(s_x1, 1)

            def b_router(c):
                g4 = lambda ap: ap.rearrange("p (g e) -> p g e", e=PER_GROUP)
                bc = lambda ap, n: ap.unsqueeze(2).to_broadcast([P, TG, n])
                dve.wait_ge(s_rexp, c + 1)
                link(V.tensor_scalar(r_den[:], r_exp[:], 1.0, None, ALU.add))
                link(V.reciprocal(r_score[:], r_den[:]))
                link(V.tensor_tensor(r_choice[:].rearrange("p (t e) -> p t e", t=TILES),
                                     r_score[:].rearrange("p (t e) -> p t e", t=TILES),
                                     bias_r[:].unsqueeze(1).to_broadcast([P, TILES, EXPERTS]), ALU.add))
                ch = g4(r_choice[:])
                V.tensor_tensor(r_hi[:], ch[:, :, 0:2], ch[:, :, 2:4], ALU.max).then_inc(s_dve, 1)
                after()
                V.tensor_tensor(r_lo[:], ch[:, :, 0:2], ch[:, :, 2:4], ALU.min).then_inc(s_dve, 1)
                dve.wait_ge(s_dve, after())
                V.tensor_tensor(r_m1[:], r_hi[:, :, 0], r_hi[:, :, 1], ALU.max).then_inc(s_dve, 1)
                after()
                V.tensor_tensor(r_mm[:], r_hi[:, :, 0], r_hi[:, :, 1], ALU.min).then_inc(s_dve, 1)
                after()
                V.tensor_tensor(r_ml[:], r_lo[:, :, 0], r_lo[:, :, 1], ALU.max).then_inc(s_dve, 1)
                dve.wait_ge(s_dve, after())
                link(V.tensor_tensor(r_m2[:], r_mm[:], r_ml[:], ALU.max))
                link(V.tensor_tensor(r_gs[:], r_m1[:], r_m2[:], ALU.add))
                gs = r_gs[:].rearrange("p (t g) -> p t g", t=TILES)
                for t in range(TILES):
                    other = gs[:, t, :].unsqueeze(1).to_broadcast([P, GROUPS, GROUPS])
                    own = gs[:, t, :].unsqueeze(2).to_broadcast([P, GROUPS, GROUPS])
                    sq = lambda ap: ap.rearrange("p (g f) -> p g f", g=GROUPS)
                    V.tensor_tensor(sq(r_ge[:, t, :]), other, own, ALU.is_ge).then_inc(s_dve, 1)
                    after()
                    V.tensor_tensor(sq(r_gt[:, t, :]), other, own, ALU.is_gt).then_inc(s_dve, 1)
                    after()
                dve.wait_ge(s_dve, chain[0])
                for t in range(TILES):
                    V.copy_predicated(r_gt[:, t, :], earlier_s[:].rearrange("p g f -> p (g f)"),
                                      r_ge[:, t, :]).then_inc(s_dve, 1)
                    after()
                dve.wait_ge(s_dve, chain[0])
                link(V.tensor_reduce(r_rank[:], r_gt[:].rearrange("p t (g f) -> p (t g) f", g=GROUPS),
                                     AX.X, ALU.add))
                link(V.tensor_scalar(r_keep[:], r_rank[:], float(TOP_GROUPS), None, ALU.is_lt))
                V.tensor_scalar(r_pen[:], r_keep[:], 1.0, -MASKED, ALU.subtract, ALU.mult).then_inc(s_dve, 1)
                after()
                V.tensor_tensor(g4(r_kept[:]), ch, bc(r_keep[:], PER_GROUP), ALU.mult).then_inc(s_dve, 1)
                dve.wait_ge(s_dve, after())
                link(V.tensor_tensor(g4(r_masked[:]), g4(r_kept[:]), bc(r_pen[:], PER_GROUP), ALU.add))
                for t in range(TILES):
                    V.max(r_top[:, t, :], r_masked[:, t * EXPERTS:(t + 1) * EXPERTS]).then_inc(s_dve, 1)
                    after()
                dve.wait_ge(s_dve, chain[0])
                link(V.memset(r_top[:, :, TOP_K:8], MASKED))
                for t in range(TILES):
                    V.match_replace(r_marked[:, t * EXPERTS:(t + 1) * EXPERTS], r_top[:, t, :],
                                    r_masked[:, t * EXPERTS:(t + 1) * EXPERTS], TAKEN).then_inc(s_dve, 1)
                    after()
                dve.wait_ge(s_dve, chain[0])
                link(V.scalar_tensor_tensor(g4(r_chosen[:]), g4(r_marked[:]), TAKEN, bc(r_keep[:], PER_GROUP),
                                            ALU.is_equal, ALU.mult))
                link(V.tensor_tensor(r_weight[:], r_chosen[:], r_score[:], ALU.mult))
                te = lambda ap: ap.rearrange("p (t e) -> p t e", t=TILES)
                link(V.tensor_reduce(r_sum[:], te(r_weight[:]), AX.X, ALU.add))
                link(V.tensor_scalar(r_sume[:], r_sum[:], 1e-20, None, ALU.add))
                link(V.reciprocal(r_rec[:], r_sume[:]))
                link(V.tensor_tensor(te(r_comb[:]), te(r_weight[:]),
                                     r_rec[:].unsqueeze(2).to_broadcast([P, TILES, EXPERTS]), ALU.mult))
                if c >= 1:
                    dve.wait_ge(s_combP, c)
                link(V.tensor_copy(r_parts[:, :, 0, :], te(r_comb[:])))
                link(V.tensor_tensor(te(r_rest[:]), te(r_comb[:]), r_parts[:, :, 0, :], ALU.subtract))
                link(V.tensor_copy(r_parts[:, :, 1, :], te(r_rest[:])))
                V.tensor_tensor(r_parts[:, :, 2, :], te(r_rest[:]), r_parts[:, :, 1, :],
                                ALU.subtract).then_inc(s_parts, 1)

            def b_hidden(c, k):
                n = STEPS * c + k
                dve.wait_ge(s_silu, n + 1)
                dve.wait_ge(s_cP, n + 1)
                V.tensor_tensor(weighted[:], gated[:, k % 2, :], psC[:], ALU.mult).then_inc(s_weighted, 1)
                dve.wait_ge(s_weighted, n + 1)
                dve.wait_ge(s_uP, n + 1)
                if n >= 2:
                    dve.wait_ge(s_down, n - 1)
                V.tensor_tensor(hid[:, k % 2, :], weighted[:], psU[:], ALU.mult).then_inc(s_hid, 1)

            def b_out(c):
                dve.wait_ge(s_down, STEPS * (c + 1))
                V.scalar_tensor_tensor(rows(c), psY[:, 0:CT], tg_moe[:, 0:1], rows(c), ALU.mult, ALU.add).then_inc(s_x2, 1)

            def c_max(c):
                dve.wait_ge(s_align, c + 1)
                if c >= 1:
                    dve.wait_ge(s_probs, TILES * c)
                V.tensor_reduce(nmax[:], psL0[:, 0:TILES * SEQ].rearrange("p (t m) -> p t m", t=TILES),
                                AX.X, ALU.max, negate=True).then_inc(s_nmax, 1)

            def c_out(c):
                dve.wait_ge(s_probs, TILES * (c + 1))
                link(V.reciprocal(prec[:], psum_e[:]))
                link(V.tensor_scalar(pgate[:], prec[:], tg[:, 1:2], None, ALU.mult))
                dve.wait_ge(s_avP, c + 1)
                for t in range(TILES):
                    r = X[:, TILES * c + t, :]
                    ins = V.scalar_tensor_tensor(r, psL0[:, CT + t * D:CT + (t + 1) * D], pgate[:, t:t + 1], r,
                                                 ALU.mult, ALU.add)
                ins.then_inc(s_x3, 1)
                dve.wait_ge(s_x3, c + 1)

            def d_out(c):
                dve.wait_ge(s_ffoutP, c + 1)
                dve.wait_ge(s_xb, c + 1)
                V.scalar_tensor_tensor(rows(c), psL0[:, 0:CT], tg[:, 3:4], xb[:], ALU.mult, ALU.add).then_inc(s_x4, 1)

            dve.wait_ge(s_tanh, 1)
            V.tensor_scalar(tg_moe[:], tg[:, 2:3], ROUTED_SCALE, None, ALU.mult).then_inc(s_dve, 1)
            after()
            for slot in range(CHUNKS + 2):
                a, b, l = slot, slot - 1, slot - 2
                A, B, C = a < CHUNKS, 0 <= b < CHUNKS, 0 <= l < CHUNKS
                if B:
                    dve.wait_ge(s_x1, b + 1)
                    norm_stats("B", b)
                if C:
                    dve.wait_ge(s_x2, l + 1)
                    norm_stats("C", l)
                if A:
                    dve.wait_ge(s_x[a], 16)
                    norm_stats("A", a)
                if B:
                    norm_apply("B", b)
                if C:
                    norm_apply("C", l)
                if A:
                    norm_apply("A", a)
                if B:
                    if b == 0:
                        dve.wait_ge(s_smallB, 64)
                    b_router(b)
                if C:
                    c_max(l)
                if A:
                    a_scores(a)
                if C:
                    c_out(l)
                    norm_stats("D", l)
                if A:
                    a_scores1(a)
                    a_softmax_shift(a)
                if B:
                    b_hidden(b, 0)
                if C:
                    norm_apply("D", l)
                if A:
                    a_softmax_norm(a)
                if B:
                    b_hidden(b, 1)
                if A:
                    a_value(a)
                if B:
                    b_hidden(b, 2)
                if A:
                    a_value1(a)
                if B:
                    b_hidden(b, 3)
                if A:
                    a_out(a)
                if B:
                    b_out(b)
                if C:
                    d_out(l)

        @block.scalar
        def _(act):
            S = nc.scalar
            act.dma_start(gates_s[:, 0:2], gates[0:1, :].partition_broadcast(P)).then_inc(s_gates, 16)
            act.dma_start(gates_s[:, 2:4], gates[1:2, :].partition_broadcast(P)).then_inc(s_gates, 16)
            act.dma_start(b2_rows[:], b2.partition_broadcast(P)).then_inc(s_gates, 16)
            act.wait_ge(s_gates, 48)
            S.activation(tg[:], gates_s[:], ACT.Tanh).then_inc(s_tanh, 1)

            def xn_copy(n, c):
                bankof = {"A": psA0, "B": psG, "C": psL0, "D": psL1}[n]
                act.wait_ge(s_xnP[n], c + 1)
                S.copy(NORM[n]["xnT"][:], bankof[:, 0:CT]).then_inc(s_xnT[n], 1)

            def a_qkv(c):
                for t, ps in enumerate((psA1, psA0)):
                    act.wait_ge(s_qkvP, TILES * c + t + 1)
                    if c >= 1:
                        act.wait_ge(s_val, TILES * c)
                    S.copy(qkv[:, t, :], ps[:, 0:3 * D]).then_inc(s_qkv, 1)

            def a_exp(c):
                act.wait_ge(s_sub, c + 1)
                S.activation(expd[:], shifted[:], ACT.Exp, scale=float(DK) ** -0.5).then_inc(s_exp, 1)

            def a_valT(c):
                act.wait_ge(s_valP, TILES * (c + 1))
                S.copy(valT[:], psA0[:, 0:CT]).then_inc(s_valT, 1)

            def b_rexp(c):
                act.wait_ge(s_logit, c + 1)
                S.activation(r_exp[:], psC[:, 0:TILES * EXPERTS], ACT.Exp, scale=-1.0).then_inc(s_rexp, 1)

            def b_combT(c):
                act.wait_ge(s_combP, c + 1)
                S.copy(combT[:], combP).then_inc(s_combT, 1)

            def b_silu(c, k):
                n = STEPS * c + k
                act.wait_ge(s_gP, n + 1)
                if n >= 2:
                    act.wait_ge(s_weighted, n - 1)
                S.activation(gated[:, k % 2, :], psG[:], ACT.Silu).then_inc(s_silu, 1)

            def c_eT(c):
                act.wait_ge(s_eP, c + 1)
                if c == 0:
                    act.wait_ge(s_late, 32)
                S.activation(eT[:], psL1[:], ACT.Identity, bias=L("bx")).then_inc(s_eT, 1)

            def c_exp(c):
                act.wait_ge(s_nmax, c + 1)
                if c >= 1:
                    act.wait_ge(s_x3, c)
                for t in range(TILES):
                    S.activation(probs[:, t, :], psL0[:, t * SEQ:(t + 1) * SEQ], ACT.Exp, bias=nmax[:, t:t + 1],
                                 accum_out=psum_e[:, t:t + 1]).then_inc(s_probs, 1)

            def c_probsT(c):
                act.wait_ge(s_probsP, c + 1)
                S.copy(probsT[:], psL1[0:SEQ, 0:CT]).then_inc(s_probsT, 1)

            def d_rankT(c):
                act.wait_ge(s_rankP, c + 1)
                S.copy(rankT[:], psL0[0:RANK, 0:CT]).then_inc(s_rankT, 1)

            def d_gelu(c):
                a, _ = LATE["b1"]
                for f in range(FF_CHUNKS):
                    act.wait_ge(s_ffP, FF_CHUNKS * c + (f // 2 + 1) * 2)
                    ps = psL1 if f < 2 else psL0
                    S.activation(ff[:, f, :], ps[:, (f % 2) * CT:(f % 2 + 1) * CT], ACT.Gelu_apprx_tanh,
                                 bias=w_late[:, a + f:a + f + 1]).then_inc(s_ff, 1)

            def d_qT(c):
                act.wait_ge(s_qP, c + 1)
                S.copy(qT[:], psL1[:, 0:CT]).then_inc(s_qT, 1)

            for slot in range(CHUNKS + 2):
                a, b, l = slot, slot - 1, slot - 2
                A, B, C = a < CHUNKS, 0 <= b < CHUNKS, 0 <= l < CHUNKS
                if B:
                    xn_copy("B", b)
                if C:
                    xn_copy("C", l)
                if A:
                    xn_copy("A", a)
                if B:
                    b_rexp(b)
                if C:
                    c_eT(l)
                if A:
                    a_qkv(a)
                if C:
                    c_exp(l)
                    c_probsT(l)
                if B:
                    b_combT(b)
                if A:
                    a_exp(a)
                if B:
                    b_silu(b, 0)
                if C:
                    xn_copy("D", l)
                    d_rankT(l)
                if B:
                    b_silu(b, 1)
                    b_silu(b, 2)
                    b_silu(b, 3)
                if A:
                    a_valT(a)
                if C:
                    d_gelu(l)
                    d_qT(l)

        @block.tensor
        def _(pe):
            T = nc.tensor
            ident = E("ident")

            def xn_transpose(n, c):
                bankof = {"A": psA0, "B": psG, "C": psL0, "D": psL1}[n]
                freed = {"A": (s_valT, c), "B": (s_silu, STEPS * c), "C": (s_x4, c), "D": (s_probsT, c + 1)}[n]
                pe.wait_ge(s_xn[n], c + 1)
                if freed[1] >= 1:
                    pe.wait_ge(*freed)
                for t in range(TILES):
                    ins = T.transpose(bankof[:, t * P:(t + 1) * P], NORM[n]["xn"][:, t * D:(t + 1) * D], ident)
                ins.then_inc(s_xnP[n], 1)

            def a_qkv(c):
                pe.wait_ge(s_xnT["A"], c + 1)
                if c >= 1:
                    pe.wait_ge(s_x1, c)
                for t, ps in enumerate((psA1, psA0)):
                    T.matmul(ps[:, 0:D], NORM["A"]["xnT"][:, t * P:(t + 1) * P], E("wq"), start=True, stop=True)
                    tok = CT * c + t * P
                    T.matmul(ps[:, D:3 * D], ctxT[:, tok:tok + P], E("wkv"), start=True, stop=True).then_inc(s_qkvP, 1)

            def a_val(c):
                for t in range(TILES):
                    pe.wait_ge(s_val, TILES * c + t + 1)
                    if t == 0:
                        pe.wait_ge(s_qkv, TILES * (c + 1))
                    T.transpose(psA0[:, t * P:(t + 1) * P], val[:, t, :], ident).then_inc(s_valP, 1)

            def a_wo(c):
                pe.wait_ge(s_valT, c + 1)
                for t in range(TILES):
                    ins = T.matmul(psA1[:, t * D:(t + 1) * D], valT[:, t * P:(t + 1) * P], E("wo"), start=True, stop=True)
                ins.then_inc(s_woP, 1)

            def b_logits(c):
                pe.wait_ge(s_xnT["B"], c + 1)
                if c >= 1:
                    pe.wait_ge(s_weighted, STEPS * c)
                for t in range(TILES):
                    ins = T.matmul(psC[:, t * EXPERTS:(t + 1) * EXPERTS], NORM["B"]["xnT"][:, t * P:(t + 1) * P],
                                   E("router"), start=True, stop=True)
                ins.then_inc(s_logit, 1)

            def b_comb(c):
                pe.wait_ge(s_parts, c + 1)
                if c >= 1:
                    pe.wait_ge(s_x2, c)
                for t in range(TILES):
                    ins = T.transpose(combP[:, t * P:(t + 1) * P],
                                      r_parts[:, t, :, :].rearrange("p a e -> p (a e)"), identb[:])
                ins.then_inc(s_combP, 1)

            def b_gate_up(c, k):
                n = STEPS * c + k
                for w, ps, done, used in ((w_gate, psG, s_gP, s_silu), (w_up, psU, s_uP, s_hid)):
                    if n >= 1:
                        pe.wait_ge(used, n)
                    for q in range(2):
                        pair = 2 * k + q
                        ins = T.matmul(ps[:, q * CT:(q + 1) * CT], w[:, pair * P:(pair + 1) * P],
                                       NORM["B"]["xnT"][:], start=True, stop=True)
                    ins.then_inc(done, 1)

            def b_spread(c, k):
                n = STEPS * c + k
                pe.wait_ge(s_combT, c + 1)
                if n >= 1:
                    pe.wait_ge(s_weighted, n)
                for q in range(2):
                    ins = T.matmul(psC[:, q * CT:(q + 1) * CT], select_s[:, 2 * k + q, :], combT[:], start=True, stop=True)
                ins.then_inc(s_cP, 1)

            def b_down(c, k):
                n = STEPS * c + k
                pe.wait_ge(s_hid, n + 1)
                for q in range(2):
                    for t in range(TILES):
                        first = k == 0 and q == 0 and t == 0
                        last = k == STEPS - 1 and q == 1 and t == TILES - 1
                        ins = T.matmul(psY[:, t * D:(t + 1) * D], hid[:, k % 2, q * CT + t * P:q * CT + (t + 1) * P],
                                       w_down[:, 2 * k + q, :], start=first, stop=last, skip_group_check=True)
                ins.then_inc(s_down, 1)

            def c_e(c):
                pe.wait_ge(s_xnT["C"], c + 1)
                if c >= 1:
                    pe.wait_ge(s_qT, c)
                T.matmul(psL1[:, 0:CT], L("wx"), NORM["C"]["xnT"][:], start=True, stop=True)
                T.matmul(psL1[:, CT:2 * CT], L("wx"), ctxT[:, CT * c:CT * (c + 1)], start=True, stop=True).then_inc(s_eP, 1)

            def c_align(c):
                pe.wait_ge(s_eT, c + 1)
                for t in range(TILES):
                    for s in range(2):
                        at = t * P + s * SEQ
                        ins = T.matmul(psL0[s * SEQ:(s + 1) * SEQ, t * SEQ:(t + 1) * SEQ], eT[:, at:at + SEQ],
                                       eT[:, CT + at:CT + at + SEQ], start=True, stop=True)
                ins.then_inc(s_align, 1)

            def c_av(c):
                pe.wait_ge(s_probs, TILES * (c + 1))
                for t in range(TILES):
                    ins = T.transpose(psL1[0:SEQ, t * P:(t + 1) * P], probs[:, t, :], ident)
                ins.then_inc(s_probsP, 1)
                pe.wait_ge(s_probsT, c + 1)
                for t in range(TILES):
                    for s in range(2):
                        at = t * P + s * SEQ
                        ins = T.matmul(psL0[s * SEQ:(s + 1) * SEQ, CT + t * D:CT + (t + 1) * D], probsT[:, at:at + SEQ],
                                       ctxM[:, 2 * (TILES * c + t) + s, :], start=True, stop=True)
                ins.then_inc(s_avP, 1)

            def d_rank(c):
                pe.wait_ge(s_xnT["D"], c + 1)
                pe.wait_ge(s_x3, c + 1)
                T.matmul(psL0[0:RANK, 0:CT], L("u1"), NORM["D"]["xnT"][:], start=True, stop=True).then_inc(s_rankP, 1)

            def d_ff(c):
                pe.wait_ge(s_rankT, c + 1)
                for f in range(FF_CHUNKS):
                    ps = psL1 if f < 2 else psL0
                    T.matmul(ps[:, (f % 2) * CT:(f % 2 + 1) * CT], w_v1[:, f * P:(f + 1) * P], rankT[:],
                             start=True, stop=True).then_inc(s_ffP, 1)

            def d_q(c):
                pe.wait_ge(s_ff, FF_CHUNKS * (c + 1))
                for f in range(FF_CHUNKS):
                    ins = T.matmul(psL1[f * RANK:(f + 1) * RANK, 0:CT], L("u2")[:, f * RANK:(f + 1) * RANK], ff[:, f, :],
                                   start=True, stop=True)
                ins.then_inc(s_qP, 1)

            def d_v2(c):
                pe.wait_ge(s_qT, c + 1)
                for t in range(TILES):
                    ins = T.matmul(psL0[:, t * D:(t + 1) * D], qT[:, t * P:(t + 1) * P], L("v2"), start=True, stop=True)
                ins.then_inc(s_ffoutP, 1)

            pe.wait_ge(s_early, 16)
            pe.wait_ge(s_ctxT, 16)
            for slot in range(CHUNKS + 2):
                a, b, l = slot, slot - 1, slot - 2
                A, B, C = a < CHUNKS, 0 <= b < CHUNKS, 0 <= l < CHUNKS
                if B:
                    xn_transpose("B", b)
                if C:
                    xn_transpose("C", l)
                if A:
                    xn_transpose("A", a)
                if B:
                    b_logits(b)
                if C:
                    if l == 0:
                        pe.wait_ge(s_late, 32)
                        pe.wait_ge(s_ctxM, 16)
                    c_e(l)
                if A:
                    a_qkv(a)
                if C:
                    c_align(l)
                if B:
                    if b == 0:
                        pe.wait_ge(s_smallB, 64)
                        pe.wait_ge(s_wgate, 16)
                        pe.wait_ge(s_wup, 16)
                        pe.wait_ge(s_wdown, 16)
                    b_gate_up(b, 0)
                if C:
                    c_av(l)
                if B:
                    b_comb(b)
                    b_spread(b, 0)
                    b_gate_up(b, 1)
                if C:
                    xn_transpose("D", l)
                    d_rank(l)
                if B:
                    b_down(b, 0)
                    b_spread(b, 1)
                    b_gate_up(b, 2)
                    b_down(b, 1)
                    b_spread(b, 2)
                if C:
                    d_ff(l)
                if B:
                    b_gate_up(b, 3)
                    b_down(b, 2)
                    b_spread(b, 3)
                if A:
                    a_val(a)
                    a_wo(a)
                if B:
                    b_down(b, 3)
                if C:
                    d_q(l)
                    d_v2(l)


def kernel(x, ctx_1024, g_xattn, g_ffn, L0_xattn_Wq, L0_xattn_Wk, L0_xattn_Wv, L0_xattn_Wo, L0_ffn_router_weight,
           L0_ffn_router_bias, L0_ffn_w_gate, L0_ffn_w_up, L0_ffn_w_down, L1_xattn_W, L1_xattn_b, L1_ffn_U1,
           L1_ffn_V1, L1_ffn_b1, L1_ffn_U2, L1_ffn_V2, L1_ffn_b2):
    import concourse.bacc as _bacc
    from concourse.bass_utils import run_bass_kernel_spmd as _run

    c = np.ascontiguousarray
    xs = c(x).reshape(TOKENS, D)
    cx = c(ctx_1024).reshape(TOKENS, D)
    early = np.concatenate([np.eye(P, dtype=xs.dtype), c(L0_xattn_Wq).T, c(L0_xattn_Wk).T, c(L0_xattn_Wv).T,
                            c(L0_xattn_Wo).T, c(L0_ffn_router_weight).T], axis=1)
    late = np.concatenate([
        c(L1_xattn_W).T, c(L1_ffn_U1),
        c(L1_ffn_U2).reshape(FF_CHUNKS, P, RANK).transpose(1, 0, 2).reshape(P, FF_CHUNKS * RANK),
        np.concatenate([c(L1_ffn_V2)] * FF_CHUNKS, axis=0),
        c(L1_xattn_b).reshape(D, 1), c(L1_ffn_b1).reshape(FF_CHUNKS, P).T], axis=1)
    experts_in = np.stack([c(w).transpose(2, 0, 1).reshape(D, EXPERTS * INNER)
                           for w in (L0_ffn_w_gate, L0_ffn_w_up)], axis=1)
    experts_out = c(L0_ffn_w_down).transpose(0, 2, 1).reshape(EXPERTS * INNER, D)
    earlier = np.zeros((P, GROUPS, GROUPS), np.int32)
    for g in range(GROUPS):
        earlier[:, g, :g] = 1
    bf16 = mybir.dt.np(BF16)
    select = np.zeros((PARTS * EXPERTS, EXPERT_PAIRS, P), bf16)
    for part in range(PARTS):
        for e in range(EXPERTS):
            select[part * EXPERTS + e, e // 2, (e % 2) * INNER:(e % 2 + 1) * INNER] = 1
    arrays = {
        "x": xs, "ctx_t": c(cx.T), "ctx_m": c(cx.reshape(TOKENS // SEQ, SEQ, D).transpose(1, 0, 2)),
        "gates": np.stack([c(g_xattn), c(g_ffn)]), "early": c(early), "late": c(late),
        "experts_in": c(experts_in), "experts_out": c(experts_out), "v1": c(L1_ffn_V1),
        "router_bias": c(L0_ffn_router_bias).reshape(1, EXPERTS), "b2": c(L1_ffn_b2).reshape(1, D),
        "earlier": earlier, "select": select, "ident_bf": np.eye(P).astype(bf16)}
    nc = _bacc.Bacc("TRN2", target_bir_lowering=False, num_devices=1)
    args = {k: nc.dram_tensor(f"in_{k}", a.shape, mybir.dt.from_np(a.dtype), kind="ExternalInput").ap()
            for k, a in arrays.items()}
    y = nc.dram_tensor("out_0", (TOKENS, D), F32, kind="ExternalOutput").ap()
    program(nc, out=y, **args)
    r = _run(nc, [{f"in_{k}": a for k, a in arrays.items()}], core_ids=[0])
    return r.results[0]["out_0"].reshape(16, SEQ, D)
```

```python
from contextlib import ExitStack

import numpy as np

import concourse.bass as bass
from concourse import mybir

F32 = mybir.dt.float32
BF16 = mybir.dt.bfloat16
ALU = mybir.AluOpType
ACT = mybir.ActivationFunctionType
AX = mybir.AxisListType

P = 128
D = 128
TOKENS = 1024
TILES = 2
CT = TILES * P
CHUNKS = TOKENS // CT
SEQ = 64
HEADS, DK = 16, 8
PAIRS_IJ = DK * DK
EXPERTS, INNER = 16, 64
GROUPS = 4
PER_GROUP = EXPERTS // GROUPS
TOP_K, TOP_GROUPS = 4, 2
EXPERT_PAIRS = EXPERTS // 2
STEPS = EXPERT_PAIRS // 2
ROUTED_SCALE = 2.5
EPS = 1e-5
MASKED, TAKEN = -1e30, -3e30
PARTS = 3
FF, RANK = 512, 32
FF_CHUNKS = FF // P

ROUTER_OPS = 28
LAG = 3
SLOTS = CHUNKS + LAG


def for_chunks(step):
    def run(*args):
        if 0 <= args[-1] < CHUNKS:
            step(*args)
    return run


_EARLY = [("ident", P), ("wkv", 2 * D), ("wq", D), ("wo", D), ("router", EXPERTS)]
_LATE = [("wx", D), ("wx_t", D), ("bx_rows", SEQ), ("u2", FF_CHUNKS * RANK), ("v2", D), ("bx", 1), ("b1", FF_CHUNKS)]


def columns(parts):
    at, out = 0, {}
    for name, n in parts:
        out[name] = (at, at + n)
        at += n
    return out, at


EARLY, EARLY_COLS = columns(_EARLY)
LATE, LATE_COLS = columns(_LATE)


def program(nc, x, ctx_t, ctx_m, gates, early, late, experts_in, experts_out, v1, router_bias, b2,
            earlier, select, ident_bf, out):
    with ExitStack() as ctx:
        def sb(name, shape, dt=F32):
            return ctx.enter_context(nc.sbuf_tensor(name, shape, dt))

        def bank(name):
            return ctx.enter_context(nc.psum_tensor(name, [P, 512], F32))

        def sem(name):
            return ctx.enter_context(nc.semaphore(name))

        psA, psB = bank("psA"), bank("psB")
        psG, psU, psC, psY = bank("psG"), bank("psU"), bank("psC"), bank("psY")
        psL0, psL1 = bank("psL0"), bank("psL1")

        w_early = sb("w_early", [P, EARLY_COLS])
        w_late = sb("w_late", [P, LATE_COLS])
        w_gate = sb("w_gate", [P, EXPERTS * INNER])
        w_up = sb("w_up", [P, EXPERTS * INNER])
        w_down = sb("w_down", [P, EXPERT_PAIRS, D])
        w_low = sb("w_low", [RANK, FF + D])
        bias_r = sb("bias_r", [P, EXPERTS])
        b2_rows = sb("b2_rows", [P, D])
        earlier_s = sb("earlier_s", [P, TILES * GROUPS * GROUPS], mybir.dt.int32)
        select_s = sb("select_s", [PARTS * EXPERTS, EXPERT_PAIRS, P], BF16)
        identb = sb("identb", [P, P], BF16)
        gates_s = sb("gates_s", [P, 4])
        tg = sb("tg", [P, 4])
        tg_moe = sb("tg_moe", [P, 1])
        b2g = sb("b2g", [P, D])
        neg_half = sb("neg_half", [P, TILES])
        zeros = sb("zeros", [P, CT])

        def E(name):
            a, b = EARLY[name]
            return w_early[:, a:b]

        def L(name):
            a, b = LATE[name]
            return w_late[:, a:b]

        X = sb("X", [P, CHUNKS * TILES, D])
        ctxT = sb("ctxT", [P, TOKENS])
        ctxM = sb("ctxM", [SEQ, TOKENS // SEQ, D])

        def norm_buffers(n):
            return dict(
                st=sb(f"st{n}", [P, TILES, 6]), mv=sb(f"mv{n}", [P, TILES, 2]),
                ve=sb(f"ve{n}", [P, TILES]), rstd=sb(f"rstd{n}", [P, TILES]),
                xn=sb(f"xn{n}", [P, CT]), xnT=sb(f"xnT{n}", [P, CT]))

        NORM = {n: norm_buffers(n) for n in "ABCD"}
        queries = sb("queries", [P, TILES, D])
        kv = sb("kv", [P, 2, TILES, 2 * D])
        prod = sb("prod", [P, TILES, HEADS * PAIRS_IJ])
        score = sb("score", [P, TILES, PAIRS_IJ])
        smax = sb("smax", [P, TILES * DK])
        shifted = sb("shifted", [P, TILES * PAIRS_IJ])
        expd = sb("expd", [P, TILES * PAIRS_IJ])
        esum = sb("esum", [P, TILES * DK])
        erec = sb("erec", [P, TILES * DK])
        attn = sb("attn", [P, TILES, PAIRS_IJ])
        prod2 = sb("prod2", [P, TILES, HEADS * PAIRS_IJ])
        val = sb("val", [P, TILES, D])
        folded = sb("folded", [P, HEADS * PAIRS_IJ // 2])
        folded2 = sb("folded2", [P, HEADS * PAIRS_IJ // 2])
        valT = sb("valT", [P, CT])

        TE, TG = TILES * EXPERTS, TILES * GROUPS
        r_exp, r_den, r_score, r_choice = (sb(n, [P, TE]) for n in ("r_exp", "r_den", "r_score", "r_choice"))
        r_pairs = sb("r_pairs", [P, TG, 6])
        r_gs = sb("r_gs", [P, TG])
        r_ge, r_gt = sb("r_ge", [P, TG * GROUPS]), sb("r_gt", [P, TG * GROUPS])
        r_rank, r_keep, r_pen = sb("r_rank", [P, TG]), sb("r_keep", [P, TG]), sb("r_pen", [P, TG])
        r_kept, r_masked = sb("r_kept", [P, TE]), sb("r_masked", [P, TE])
        r_top = sb("r_top", [P, TILES, 8])
        r_marked, r_weight = sb("r_marked", [P, TE]), sb("r_weight", [P, TE])
        r_sum, r_sume, r_rec = (sb(n, [P, TILES]) for n in ("r_sum", "r_sume", "r_rec"))
        r_comb, r_rest = sb("r_comb", [P, TE]), sb("r_rest", [P, TE])
        r_parts = sb("r_parts", [P, TILES, PARTS, EXPERTS], BF16)
        combT = sb("combT", [PARTS * EXPERTS, CT], BF16)
        gated = sb("gated", [P, 2, 2 * CT])
        glu = sb("glu", [P, STEPS, 2 * CT])
        hid = sb("hid", [P, 2, 2 * CT])

        eoT = sb("eoT", [P, CT])
        keysT = sb("keysT", [P, CT])
        w_ff = sb("w_ff", [P, FF])
        nmax = sb("nmax", [P, TILES])
        psum_e = sb("psum_e", [P, TILES])
        probs = sb("probs", [P, TILES, SEQ])
        prec = sb("prec", [P, TILES])
        pgate = sb("pgate", [P, TILES])
        probsT = sb("probsT", [SEQ, CT])

        xb = sb("xb", [P, CT])
        ff = sb("ff", [P, FF_CHUNKS, CT])
        qT = sb("qT", [P, CT])

        s_x = [sem(f"s_xin{c}") for c in range(CHUNKS)]
        s_early = [sem("s_early0"), sem("s_early1")]
        s_ctxT = [sem("s_ctxT0"), sem("s_ctxT1")]
        s_ctxM, s_gates = sem("s_ctxM"), sem("s_gates")
        s_smallB, s_wgate, s_wup, s_wdown, s_late = (
            sem("s_smallB"), sem("s_wgate"), sem("s_wup"), sem("s_wdown"), sem("s_late"))
        s_out = sem("s_out")
        s_tanh, s_b2g, s_moe_gate, s_zero = sem("s_tanh"), sem("s_b2g"), sem("s_moe_gate"), sem("s_zero")
        s_pool = sem("s_pool")
        s_stats = {n: sem(f"s_stats{n}") for n in "ABCD"}
        s_rstd = {n: sem(f"s_rstd{n}") for n in "ABCD"}
        s_xn = {n: sem(f"s_xn{n}") for n in "ABCD"}
        s_xnP = {n: sem(f"s_xnP{n}") for n in "ABCD"}
        s_xnT = {n: sem(f"s_xnT{n}") for n in "ABCD"}
        s_kvP, s_kv, s_queryP, s_query = sem("s_kvP"), sem("s_kv"), sem("s_queryP"), sem("s_query")
        s_score, s_eoP, s_eoT = sem("s_score"), sem("s_eoP"), sem("s_eoT")
        s_folded, s_sub, s_exp, s_attn, s_vfolded, s_val = (
            sem("s_folded"), sem("s_sub"), sem("s_exp"), sem("s_attn"), sem("s_vfolded"), sem("s_val"))
        s_valP, s_valT, s_woP, s_x1 = sem("s_valP"), sem("s_valT"), sem("s_woP"), sem("s_x1")
        s_logit, s_rexp, s_parts, s_combP, s_combT = (
            sem("s_logit"), sem("s_rexp"), sem("s_parts"), sem("s_combP"), sem("s_combT"))
        s_gP, s_uP, s_cP, s_silu, s_glu, s_hid, s_down = (
            sem("s_gP"), sem("s_uP"), sem("s_cP"), sem("s_silu"), sem("s_glu"), sem("s_hid"), sem("s_down"))
        s_x2 = sem("s_x2")
        s_bnstats = {n: sem(f"s_bnstats{n}") for n in "ABCD"}
        s_router, s_prod1, s_vprod1, s_prod0, s_smax, s_esum, s_erec, s_vprod0, s_prec, s_pgate = (sem(x) for x in (
            "s_router", "s_prod1", "s_vprod1", "s_prod0", "s_smax", "s_esum", "s_erec", "s_vprod0", "s_prec", "s_pgate"))
        s_keysP, s_keysT, s_align, s_nmax, s_probs, s_probsP, s_probsT, s_avP, s_x3 = (
            sem("s_keysP"), sem("s_keysT"), sem("s_align"), sem("s_nmax"), sem("s_probs"), sem("s_probsP"),
            sem("s_probsT"), sem("s_avP"), sem("s_x3"))
        s_wffP, s_wff, s_ffP, s_ff, s_qP, s_qT, s_ffoutP, s_xb, s_x4 = (
            sem("s_wffP"), sem("s_wff"), sem("s_ffP"), sem("s_ff"), sem("s_qP"), sem("s_qT"),
            sem("s_ffoutP"), sem("s_xb"), sem("s_x4"))

        block = ctx.enter_context(nc.Block())

        def rows(c):
            return X[:, TILES * c:TILES * (c + 1), :].rearrange("p t d -> p (t d)")

        combP = psB[0:PARTS * EXPERTS, 0:CT // 2].bitcast(BF16)

        def score_product(engine, c, t):
            q = queries[:, t, :].rearrange("p (i h) -> p i h", h=HEADS).unsqueeze(2)
            k = kv[:, c % 2, t, 0:D].rearrange("p (j h) -> p j h", h=HEADS).unsqueeze(1)
            shape = [P, DK, DK, HEADS]
            return engine.tensor_tensor(prod[:, t, :].rearrange("p (i j h) -> p i j h", i=DK, j=DK),
                                        q.to_broadcast(shape), k.to_broadcast(shape), ALU.mult)

        def value_product(engine, c, t):
            a = attn[:, t, :].rearrange("p (i j) -> p i j", i=DK).unsqueeze(1)
            v = kv[:, c % 2, t, D:2 * D].rearrange("p (h j) -> p h j", h=HEADS).unsqueeze(2)
            shape = [P, HEADS, DK, DK]
            return engine.tensor_tensor(prod2[:, t, :].rearrange("p (h i j) -> p h i j", h=HEADS, i=DK),
                                        a.to_broadcast(shape), v.to_broadcast(shape), ALU.mult)

        @block.sync
        def _(sp):
            xv = x.rearrange("(n p) d -> p n d", p=P)
            sp.dma_start(X[:, 0:TILES, :], xv[:, 0:TILES, :]).then_inc(s_x[0], 16)
            sp.dma_start(ctxT[:, 0:CT], ctx_t[:, 0:CT]).then_inc(s_ctxT[0], 16)
            for c in range(1, CHUNKS):
                sp.dma_start(X[:, TILES * c:TILES * (c + 1), :],
                             xv[:, TILES * c:TILES * (c + 1), :]).then_inc(s_x[c], 16)
                if c == 1:
                    sp.dma_start(ctxT[:, CT:], ctx_t[:, CT:]).then_inc(s_ctxT[1], 16)
            sp.dma_start(bias_r[:], router_bias.partition_broadcast(P)).then_inc(s_smallB, 16)
            sp.dma_start(earlier_s[:], earlier).then_inc(s_smallB, 16)
            sp.dma_start(select_s[:], select).then_inc(s_smallB, 16)
            sp.dma_start(identb[:], ident_bf).then_inc(s_smallB, 16)
            sp.dma_start(w_gate[:], experts_in[:, 0, :]).then_inc(s_wgate, 16)
            sp.dma_start(w_up[:], experts_in[:, 1, :]).then_inc(s_wup, 16)
            sp.dma_start(w_down[:], experts_out.rearrange("(n p) d -> p n d", p=P)).then_inc(s_wdown, 16)
            sp.dma_start(w_late[:], late).then_inc(s_late, 16)
            sp.dma_start(w_low[:], v1).then_inc(s_late, 16)
            sp.dma_start(ctxM[:], ctx_m).then_inc(s_ctxM, 16)
            ov = out.rearrange("(n p) d -> p n d", p=P)
            for c in range(CHUNKS):
                sp.wait_ge(s_x4, c + 1)
                sp.dma_start(ov[:, TILES * c:TILES * (c + 1), :],
                             X[:, TILES * c:TILES * (c + 1), :]).then_inc(s_out, 16)
            sp.wait_ge(s_out, 16 * CHUNKS)

        @block.gpsimd
        def _(pool):
            chain = [0]

            def link(ins):
                chain[0] += 1
                ins.then_inc(s_pool, 1)
                pool.wait_ge(s_pool, chain[0])

            nc.gpsimd.memset(zeros[:], 0.0).then_inc(s_zero, 1)
            link(nc.gpsimd.memset(neg_half[:], -0.5))

            @for_chunks
            def rstd(n, c):
                b = NORM[n]
                pool.wait_ge(s_stats[n], c + 1)
                link(nc.gpsimd.tensor_scalar(b["ve"][:], b["mv"][:, :, 1], EPS, None, ALU.add))
                nc.gpsimd.tensor_tensor(b["rstd"][:], b["ve"][:], neg_half[:], ALU.pow).then_inc(s_rstd[n], 1)
                if n != "A":
                    pool.wait_ge(s_rstd[n], c + 1)
                    if c >= 1:
                        pool.wait_ge(s_xnP[n], c)
                    nc.gpsimd.tensor_scalar(b["xn"][:, D:CT], X[:, TILES * c + 1, :], b["mv"][:, 1, 0:1],
                                            b["rstd"][:, 1:2], ALU.subtract, ALU.mult).then_inc(s_xn[n], 1)

            @for_chunks
            def attn_product(c):
                pool.wait_ge(s_query, TILES * c + 2)
                pool.wait_ge(s_kv, c + 1)
                score_product(nc.gpsimd, c, 1).then_inc(s_prod1, 1)

            @for_chunks
            def attn_fold(c):
                pool.wait_ge(s_prod1, c + 1)
                if c >= 1:
                    pool.wait_ge(s_score, TILES * c)
                p = prod[:, 1, :].rearrange("p (a h) -> p a h", h=HEADS)
                nc.gpsimd.tensor_tensor(folded[:].rearrange("p (a h) -> p a h", h=HEADS // 2), p[:, :, 0:HEADS // 2],
                                        p[:, :, HEADS // 2:], ALU.add).then_inc(s_folded, 1)

            @for_chunks
            def attn_value_product(c):
                pool.wait_ge(s_attn, c + 1)
                value_product(nc.gpsimd, c, 1).then_inc(s_vprod1, 1)

            @for_chunks
            def value_fold(c):
                pool.wait_ge(s_vprod1, c + 1)
                if c >= 1:
                    pool.wait_ge(s_val, TILES * c)
                p = prod2[:, 1, :].rearrange("p (a j) -> p a j", j=DK)
                nc.gpsimd.tensor_tensor(folded2[:].rearrange("p (a j) -> p a j", j=DK // 2), p[:, :, 0:DK // 2],
                                        p[:, :, DK // 2:], ALU.add).then_inc(s_vfolded, 1)

            @for_chunks
            def add_b2(c):
                pool.wait_ge(s_x3, c + 1)
                if c >= 1:
                    pool.wait_ge(s_x4, c)
                if c == 0:
                    pool.wait_ge(s_gates, 48)
                    pool.wait_ge(s_tanh, 1)
                    nc.gpsimd.tensor_scalar(b2g[:], b2_rows[:], tg[:, 3:4], None, ALU.mult).then_inc(s_b2g, 1)
                    pool.wait_ge(s_b2g, 1)
                nc.gpsimd.tensor_tensor(xb[:].rearrange("p (t d) -> p t d", t=TILES),
                                        X[:, TILES * c:TILES * (c + 1), :],
                                        b2g[:].unsqueeze(1).to_broadcast([P, TILES, D]), ALU.add).then_inc(s_xb, 1)

            for slot in range(SLOTS):
                c0, c1, c2, c3 = slot, slot - 1, slot - 2, slot - 3
                attn_value_product(c1)
                value_fold(c1)
                rstd("A", c0)
                rstd("B", c1)
                rstd("D", c3)
                attn_product(c0)
                attn_fold(c0)
                add_b2(c3)
                rstd("C", c2)

        @block.vector
        def _(dve):
            V = nc.vector

            def by_tile(ap):
                return ap.rearrange("p (t e) -> p t e", t=TILES)

            def by_group(ap):
                return ap.rearrange("p (g e) -> p g e", e=PER_GROUP)

            @for_chunks
            def norm_stats(n, c):
                b = NORM[n]
                dve.wait_ge(*{"A": (s_x[c], 16), "B": (s_x1, c + 1), "C": (s_x2, c + 1), "D": (s_x3, c + 1)}[n])
                for t in range(TILES):
                    V.bn_stats(b["st"][:, t, :], X[:, TILES * c + t, :]).then_inc(s_bnstats[n], 1)

            @for_chunks
            def norm_aggregate(n, c):
                b = NORM[n]
                dve.wait_ge(s_bnstats[n], TILES * (c + 1))
                for t in range(TILES):
                    ins = V.bn_aggr(b["mv"][:, t, :], b["st"][:, t, :])
                ins.then_inc(s_stats[n], 1)

            @for_chunks
            def norm_apply(n, c):
                b = NORM[n]
                if n != "A":
                    dve.wait_ge(s_rstd[n], c + 1)
                dve.wait_ge(s_stats[n], c + 1)
                if c >= 1:
                    dve.wait_ge(s_xnP[n], c)
                if n == "A":
                    for t in range(TILES):
                        V.tensor_scalar(b["xn"][:, t * D:(t + 1) * D], X[:, TILES * c + t, :],
                                        b["mv"][:, t, 0:1], None, ALU.subtract).then_inc(s_xn[n], 1)
                else:
                    V.tensor_scalar(b["xn"][:, 0:D], X[:, TILES * c, :], b["mv"][:, 0, 0:1], b["rstd"][:, 0:1],
                                    ALU.subtract, ALU.mult).then_inc(s_xn[n], 1)

            @for_chunks
            def a_score_product(c):
                dve.wait_ge(s_query, TILES * c + 1)
                dve.wait_ge(s_kv, c + 1)
                score_product(V, c, 0).then_inc(s_prod0, 1)

            @for_chunks
            def a_scores0(c):
                dve.wait_ge(s_prod0, c + 1)
                V.tensor_reduce(score[:, 0, :], prod[:, 0, :].rearrange("p (a h) -> p a h", h=HEADS),
                                AX.X, ALU.add).then_inc(s_score, 1)

            @for_chunks
            def a_scores1(c):
                dve.wait_ge(s_folded, c + 1)
                V.tensor_reduce(score[:, 1, :], folded[:].rearrange("p (a h) -> p a h", h=HEADS // 2),
                                AX.X, ALU.add).then_inc(s_score, 1)

            @for_chunks
            def a_softmax_max(c):
                dve.wait_ge(s_score, TILES * (c + 1))
                V.tensor_reduce(smax[:], score[:].rearrange("p t (i j) -> p (t i) j", i=DK), AX.X, ALU.max).then_inc(s_smax, 1)

            @for_chunks
            def a_softmax_shift(c):
                sc = score[:].rearrange("p t (i j) -> p (t i) j", i=DK)
                dve.wait_ge(s_smax, c + 1)
                if c >= 1:
                    dve.wait_ge(s_exp, c)
                V.tensor_tensor(shifted[:].rearrange("p (a j) -> p a j", j=DK), sc,
                                smax[:].unsqueeze(2).to_broadcast([P, TILES * DK, DK]), ALU.subtract).then_inc(s_sub, 1)

            @for_chunks
            def a_softmax_sum(c):
                dve.wait_ge(s_exp, c + 1)
                V.tensor_reduce(esum[:], expd[:].rearrange("p (a j) -> p a j", j=DK), AX.X, ALU.add).then_inc(s_esum, 1)

            @for_chunks
            def a_softmax_rec(c):
                dve.wait_ge(s_esum, c + 1)
                V.reciprocal(erec[:], esum[:]).then_inc(s_erec, 1)

            @for_chunks
            def a_softmax_norm(c):
                dve.wait_ge(s_erec, c + 1)
                ex = expd[:].rearrange("p (a j) -> p a j", j=DK)
                V.tensor_tensor(attn[:].rearrange("p t (i j) -> p (t i) j", i=DK), ex,
                                erec[:].unsqueeze(2).to_broadcast([P, TILES * DK, DK]), ALU.mult).then_inc(s_attn, 1)

            @for_chunks
            def a_value_product(c):
                dve.wait_ge(s_attn, c + 1)
                value_product(V, c, 0).then_inc(s_vprod0, 1)

            @for_chunks
            def a_value0(c):
                dve.wait_ge(s_vprod0, c + 1)
                if c >= 1:
                    dve.wait_ge(s_valP, TILES * c)
                V.tensor_reduce(val[:, 0, :], prod2[:, 0, :].rearrange("p (a j) -> p a j", j=DK),
                                AX.X, ALU.add).then_inc(s_val, 1)

            @for_chunks
            def a_value1(c):
                dve.wait_ge(s_vfolded, c + 1)
                V.tensor_reduce(val[:, 1, :], folded2[:].rearrange("p (a j) -> p a j", j=DK // 2),
                                AX.X, ALU.add).then_inc(s_val, 1)

            @for_chunks
            def a_out(c):
                if c == 0:
                    dve.wait_ge(s_tanh, 1)
                    V.tensor_scalar(tg_moe[:], tg[:, 2:3], ROUTED_SCALE, None, ALU.mult).then_inc(s_moe_gate, 1)
                dve.wait_ge(s_woP, c + 1)
                V.scalar_tensor_tensor(rows(c), psA[:, 0:CT], tg[:, 0:1], rows(c), ALU.mult, ALU.add).then_inc(s_x1, 1)

            def after(c, n):
                dve.wait_ge(s_router, ROUTER_OPS * c + n)

            @for_chunks
            def b_sigmoid_denominator(c):
                if c == 0:
                    dve.wait_ge(s_smallB, 64)
                dve.wait_ge(s_rexp, c + 1)
                V.tensor_scalar(r_den[:], r_exp[:], 1.0, None, ALU.add).then_inc(s_router, 1)

            @for_chunks
            def b_sigmoid(c):
                after(c, 1)
                V.reciprocal(r_score[:], r_den[:]).then_inc(s_router, 1)

            @for_chunks
            def b_choice_scores(c):
                after(c, 2)
                V.tensor_tensor(by_tile(r_choice[:]), by_tile(r_score[:]),
                                bias_r[:].unsqueeze(1).to_broadcast([P, TILES, EXPERTS]), ALU.add).then_inc(s_router, 1)

            @for_chunks
            def b_pair_sums(c):
                after(c, 3)
                ch = by_group(r_choice[:])
                V.tensor_tensor(r_pairs[:, :, 0:3], ch[:, :, 0:3], ch[:, :, 1:4], ALU.add).then_inc(s_router, 1)
                V.tensor_tensor(r_pairs[:, :, 3:5], ch[:, :, 0:2], ch[:, :, 2:4], ALU.add).then_inc(s_router, 1)
                V.tensor_tensor(r_pairs[:, :, 5:6], ch[:, :, 0:1], ch[:, :, 3:4], ALU.add).then_inc(s_router, 1)

            @for_chunks
            def b_group_scores(c):
                after(c, 6)
                V.tensor_reduce(r_gs[:], r_pairs[:], AX.X, ALU.max).then_inc(s_router, 1)

            @for_chunks
            def b_group_beats(c):
                after(c, 7)
                gs = by_tile(r_gs[:])
                other = gs.unsqueeze(2).to_broadcast([P, TILES, GROUPS, GROUPS])
                own = gs.unsqueeze(3).to_broadcast([P, TILES, GROUPS, GROUPS])
                square = lambda ap: ap.rearrange("p (t g f) -> p t g f", t=TILES, g=GROUPS)
                V.tensor_tensor(square(r_ge[:]), other, own, ALU.is_ge).then_inc(s_router, 1)
                V.tensor_tensor(square(r_gt[:]), other, own, ALU.is_gt).then_inc(s_router, 1)

            @for_chunks
            def b_group_ties(c):
                after(c, 9)
                V.copy_predicated(r_gt[:], earlier_s[:], r_ge[:]).then_inc(s_router, 1)

            @for_chunks
            def b_group_ranks(c):
                after(c, 10)
                V.tensor_reduce(r_rank[:], r_gt[:].rearrange("p (a f) -> p a f", f=GROUPS), AX.X,
                                ALU.add).then_inc(s_router, 1)

            @for_chunks
            def b_group_masks(c):
                after(c, 11)
                V.tensor_scalar(r_pen[:], r_rank[:], float(TOP_GROUPS), MASKED, ALU.is_ge, ALU.mult).then_inc(s_router, 1)
                V.tensor_scalar(r_keep[:], r_rank[:], float(TOP_GROUPS), None, ALU.is_lt).then_inc(s_router, 1)

            spread = lambda ap: ap.unsqueeze(2).to_broadcast([P, TG, PER_GROUP])

            @for_chunks
            def b_mask_experts(c):
                after(c, 13)
                V.tensor_tensor(by_group(r_masked[:]), by_group(r_choice[:]), spread(r_pen[:]), ALU.add).then_inc(s_router, 1)
                V.tensor_tensor(by_group(r_kept[:]), by_group(r_score[:]), spread(r_keep[:]), ALU.mult).then_inc(s_router, 1)

            @for_chunks
            def b_top_experts(c):
                after(c, 15)
                for t in range(TILES):
                    V.max(r_top[:, t, :], r_masked[:, t * EXPERTS:(t + 1) * EXPERTS]).then_inc(s_router, 1)

            @for_chunks
            def b_cut_top(c):
                after(c, 17)
                V.memset(r_top[:, :, TOP_K:8], MASKED).then_inc(s_router, 1)

            @for_chunks
            def b_mark_chosen(c):
                after(c, 18)
                for t in range(TILES):
                    V.match_replace(r_marked[:, t * EXPERTS:(t + 1) * EXPERTS], r_top[:, t, :],
                                    r_masked[:, t * EXPERTS:(t + 1) * EXPERTS], TAKEN).then_inc(s_router, 1)

            @for_chunks
            def b_chosen_weights(c):
                after(c, 20)
                for t in range(TILES):
                    span = slice(t * EXPERTS, (t + 1) * EXPERTS)
                    V.scalar_tensor_tensor(r_weight[:, span], r_marked[:, span], TAKEN, r_kept[:, span],
                                           ALU.is_equal, ALU.mult, accum_out=r_sum[:, t:t + 1]).then_inc(s_router, 1)

            @for_chunks
            def b_weight_sum(c):
                after(c, 22)
                V.tensor_scalar(r_sume[:], r_sum[:], 1e-20, None, ALU.add).then_inc(s_router, 1)

            @for_chunks
            def b_sum_reciprocal(c):
                after(c, 23)
                V.reciprocal(r_rec[:], r_sume[:]).then_inc(s_router, 1)

            rec = r_rec[:].unsqueeze(2).to_broadcast([P, TILES, EXPERTS])

            @for_chunks
            def b_weights_high(c):
                after(c, 24)
                if c >= 1:
                    dve.wait_ge(s_combP, c)
                V.tensor_tensor(by_tile(r_comb[:]), by_tile(r_weight[:]), rec, ALU.mult).then_inc(s_router, 1)
                V.tensor_tensor(r_parts[:, :, 0, :], by_tile(r_weight[:]), rec, ALU.mult).then_inc(s_router, 1)

            @for_chunks
            def b_weights_middle(c):
                after(c, 26)
                V.tensor_tensor(by_tile(r_rest[:]), by_tile(r_comb[:]), r_parts[:, :, 0, :], ALU.subtract).then_inc(s_router, 1)
                V.tensor_tensor(r_parts[:, :, 1, :], by_tile(r_comb[:]), r_parts[:, :, 0, :], ALU.subtract).then_inc(s_router, 1)

            @for_chunks
            def b_weights_low(c):
                after(c, 28)
                V.tensor_tensor(r_parts[:, :, 2, :], by_tile(r_rest[:]), r_parts[:, :, 1, :],
                                ALU.subtract).then_inc(s_parts, 1)

            @for_chunks
            def b_glu(k, c):
                n = STEPS * c + k
                dve.wait_ge(s_silu, n + 1)
                dve.wait_ge(s_uP, n + 1)
                if c >= 1:
                    dve.wait_ge(s_hid, n + 1 - STEPS)
                V.tensor_tensor(glu[:, k, :], gated[:, k % 2, :], psU[:], ALU.mult).then_inc(s_glu, 1)

            @for_chunks
            def b_hidden(k, c):
                n = STEPS * c + k
                dve.wait_ge(s_cP, n + 1)
                dve.wait_ge(s_glu, n + 1)
                if n >= 2:
                    dve.wait_ge(s_down, n - 1)
                V.tensor_tensor(hid[:, k % 2, :], glu[:, k, :], psC[:], ALU.mult).then_inc(s_hid, 1)

            @for_chunks
            def b_out(c):
                if c == 0:
                    dve.wait_ge(s_moe_gate, 1)
                dve.wait_ge(s_down, STEPS * (c + 1))
                V.scalar_tensor_tensor(rows(c), psY[:, 0:CT], tg_moe[:, 0:1], rows(c), ALU.mult, ALU.add).then_inc(s_x2, 1)

            @for_chunks
            def c_max(c):
                dve.wait_ge(s_align, c + 1)
                if c >= 1:
                    dve.wait_ge(s_probs, TILES * c)
                V.tensor_reduce(nmax[:], psL0[:, 0:TILES * SEQ].rearrange("p (t m) -> p t m", t=TILES),
                                AX.X, ALU.max, negate=True).then_inc(s_nmax, 1)

            @for_chunks
            def c_sum_reciprocal(c):
                dve.wait_ge(s_probs, TILES * (c + 1))
                V.reciprocal(prec[:], psum_e[:]).then_inc(s_prec, 1)

            @for_chunks
            def c_gate(c):
                dve.wait_ge(s_prec, c + 1)
                V.tensor_scalar(pgate[:], prec[:], tg[:, 1:2], None, ALU.mult).then_inc(s_pgate, 1)

            @for_chunks
            def c_out(c):
                dve.wait_ge(s_avP, c + 1)
                dve.wait_ge(s_pgate, c + 1)
                for t in range(TILES):
                    r = X[:, TILES * c + t, :]
                    ins = V.scalar_tensor_tensor(r, psL0[:, CT + t * D:CT + (t + 1) * D], pgate[:, t:t + 1], r,
                                                 ALU.mult, ALU.add)
                ins.then_inc(s_x3, 1)

            @for_chunks
            def d_out(c):
                dve.wait_ge(s_ffoutP, c + 1)
                dve.wait_ge(s_xb, c + 1)
                V.scalar_tensor_tensor(rows(c), psL0[:, 0:CT], tg[:, 3:4], xb[:], ALU.mult, ALU.add).then_inc(s_x4, 1)

            for slot in range(SLOTS):
                c0, c1, c2, c3 = slot, slot - 1, slot - 2, slot - 3
                norm_stats("A", c0)
                b_sum_reciprocal(c2)
                b_glu(0, c2)
                b_weights_high(c2)
                norm_aggregate("A", c0)
                b_weights_middle(c2)
                norm_apply("C", c3)
                b_weights_low(c2)
                a_value_product(c1)
                b_glu(1, c2)
                a_value0(c1)
                c_max(c3)
                a_value1(c1)
                b_hidden(0, c2)
                norm_apply("A", c0)
                c_sum_reciprocal(c3)
                c_gate(c3)
                b_hidden(1, c2)
                a_out(c1)
                norm_stats("B", c1)
                norm_aggregate("B", c1)
                c_out(c3)
                b_glu(2, c2)
                norm_stats("D", c3)
                norm_apply("B", c1)
                norm_aggregate("D", c3)
                b_hidden(2, c2)
                a_score_product(c0)
                norm_apply("D", c3)
                b_glu(3, c2)
                a_scores0(c0)
                b_sigmoid_denominator(c1)
                b_hidden(3, c2)
                b_sigmoid(c1)
                b_choice_scores(c1)
                b_pair_sums(c1)
                b_group_scores(c1)
                b_group_beats(c1)
                a_scores1(c0)
                b_group_ties(c1)
                a_softmax_max(c0)
                b_group_ranks(c1)
                a_softmax_shift(c0)
                b_group_masks(c1)
                b_out(c2)
                b_mask_experts(c1)
                a_softmax_sum(c0)
                norm_stats("C", c2)
                b_top_experts(c1)
                norm_aggregate("C", c2)
                b_cut_top(c1)
                b_mark_chosen(c1)
                a_softmax_rec(c0)
                b_chosen_weights(c1)
                a_softmax_norm(c0)
                b_weight_sum(c1)
                d_out(c3)

        @block.scalar
        def _(act):
            S = nc.scalar
            act.dma_start(w_early[:, 0:3 * P], early[:, 0:3 * P]).then_inc(s_early[0], 16)
            act.dma_start(w_early[:, 3 * P:], early[:, 3 * P:]).then_inc(s_early[1], 16)
            act.dma_start(gates_s[:, 0:2], gates[0:1, :].partition_broadcast(P)).then_inc(s_gates, 16)
            act.dma_start(gates_s[:, 2:4], gates[1:2, :].partition_broadcast(P)).then_inc(s_gates, 16)
            act.dma_start(b2_rows[:], b2.partition_broadcast(P)).then_inc(s_gates, 16)

            @for_chunks
            def xn_copy(n, c):
                bankof = {"A": psA, "B": psB, "C": psL1, "D": psL1}[n]
                act.wait_ge(s_xnP[n], c + 1)
                if n == "B" and c >= 1:
                    act.wait_ge(s_uP, STEPS * c)
                S.copy(NORM[n]["xnT"][:], bankof[:, 0:CT]).then_inc(s_xnT[n], 1)

            def a_kv(c):
                act.wait_ge(s_kvP, c + 1)
                if c >= 2:
                    act.wait_ge(s_val, TILES * (c - 1))
                S.copy(kv[:, c % 2, :, :], psA[:].rearrange("p (t d) -> p t d", t=TILES)).then_inc(s_kv, 1)

            @for_chunks
            def a_kv_next(c):
                if c + 1 < CHUNKS:
                    a_kv(c + 1)

            @for_chunks
            def a_q(c):
                act.wait_ge(s_queryP, c + 1)
                act.wait_ge(s_rstd["A"], c + 1)
                if c >= 1:
                    act.wait_ge(s_score, TILES * c)
                for t in range(TILES):
                    S.activation(queries[:, t, :], psA[:, CT + t * D:CT + (t + 1) * D], ACT.Copy,
                                 scale=NORM["A"]["rstd"][:, t:t + 1]).then_inc(s_query, 1)

            @for_chunks
            def a_exp(c):
                act.wait_ge(s_sub, c + 1)
                if c == 0:
                    act.wait_ge(s_gates, 48)
                    S.activation(tg[:], gates_s[:], ACT.Tanh).then_inc(s_tanh, 1)
                S.activation(expd[:], shifted[:], ACT.Exp, scale=float(DK) ** -0.5).then_inc(s_exp, 1)

            @for_chunks
            def a_valT(c):
                act.wait_ge(s_valP, TILES * (c + 1))
                S.copy(valT[:], psA[:, 0:CT]).then_inc(s_valT, 1)

            @for_chunks
            def b_rexp(c):
                act.wait_ge(s_logit, c + 1)
                if c >= 1:
                    act.wait_ge(s_router, ROUTER_OPS * (c - 1) + 1)
                S.activation(r_exp[:], psB[:, 0:TILES * EXPERTS], ACT.Exp, scale=-1.0).then_inc(s_rexp, 1)

            @for_chunks
            def b_combT(c):
                act.wait_ge(s_combP, c + 1)
                if c >= 1:
                    act.wait_ge(s_cP, STEPS * c)
                S.copy(combT[:], combP).then_inc(s_combT, 1)

            @for_chunks
            def b_silu(k, c):
                n = STEPS * c + k
                act.wait_ge(s_gP, n + 1)
                if n >= 2:
                    act.wait_ge(s_glu, n - 1)
                S.activation(gated[:, k % 2, :], psG[:], ACT.Silu).then_inc(s_silu, 1)

            @for_chunks
            def c_eoT(c):
                act.wait_ge(s_eoP, c + 1)
                if c == 0:
                    act.wait_ge(s_late, 32)
                if c >= 1:
                    act.wait_ge(s_align, c)
                S.activation(eoT[:], psL1[:, CT:2 * CT], ACT.Identity, bias=L("bx")).then_inc(s_eoT, 1)

            @for_chunks
            def c_keysT(c):
                act.wait_ge(s_keysP, c + 1)
                S.copy(keysT[:], psL1[:, 0:CT]).then_inc(s_keysT, 1)

            @for_chunks
            def c_exp(c):
                act.wait_ge(s_nmax, c + 1)
                if c >= 1:
                    act.wait_ge(s_x3, c)
                for t in range(TILES):
                    S.activation(probs[:, t, :], psL0[:, t * SEQ:(t + 1) * SEQ], ACT.Exp, bias=nmax[:, t:t + 1],
                                 accum_out=psum_e[:, t:t + 1]).then_inc(s_probs, 1)

            @for_chunks
            def c_probsT(c):
                act.wait_ge(s_probsP, c + 1)
                S.copy(probsT[:], psL1[0:SEQ, 0:CT]).then_inc(s_probsT, 1)

            @for_chunks
            def d_weights(c):
                if c == 0:
                    act.wait_ge(s_wffP, 1)
                    S.copy(w_ff[:], psL1[:]).then_inc(s_wff, 1)

            @for_chunks
            def d_gelu(c):
                a, _ = LATE["b1"]
                for f in range(FF_CHUNKS):
                    act.wait_ge(s_ffP, FF_CHUNKS * c + (f // 2 + 1) * 2)
                    ps = psL1 if f < 2 else psL0
                    S.activation(ff[:, f, :], ps[:, (f % 2) * CT:(f % 2 + 1) * CT], ACT.Gelu_apprx_tanh,
                                 bias=w_late[:, a + f:a + f + 1]).then_inc(s_ff, 1)

            @for_chunks
            def d_qT(c):
                act.wait_ge(s_qP, c + 1)
                S.copy(qT[:], psL1[:, 0:CT]).then_inc(s_qT, 1)

            a_kv(0)
            for slot in range(SLOTS):
                c0, c1, c2, c3 = slot, slot - 1, slot - 2, slot - 3
                a_valT(c1)
                c_probsT(c3)
                b_silu(2, c2)
                d_weights(c1)
                xn_copy("A", c0)
                a_q(c0)
                b_silu(3, c2)
                xn_copy("B", c1)
                b_rexp(c1)
                xn_copy("D", c3)
                d_gelu(c3)
                a_exp(c0)
                d_qT(c3)
                b_silu(0, c1)
                c_eoT(c2)
                a_kv_next(c0)
                c_keysT(c2)
                b_silu(1, c1)
                b_combT(c1)
                xn_copy("C", c2)
                c_exp(c2)

        @block.tensor
        def _(pe):
            T = nc.tensor
            ident = E("ident")

            @for_chunks
            def xn_transpose(n, c):
                bankof = {"A": psA, "B": psB, "C": psL1, "D": psL1}[n]
                freed = {"A": (s_x1, c), "B": (s_combT, c), "C": (s_keysT, c + 1), "D": (s_probsT, c + 1)}[n]
                pe.wait_ge(s_xn[n], TILES * (c + 1))
                if n == "A" and c == 0:
                    pe.wait_ge(s_kv, 1)
                if freed[1] >= 1:
                    pe.wait_ge(*freed)
                for t in range(TILES):
                    ins = T.transpose(bankof[:, t * P:(t + 1) * P], NORM[n]["xn"][:, t * D:(t + 1) * D], ident)
                ins.then_inc(s_xnP[n], 1)

            def a_kv(c):
                if c <= 1:
                    pe.wait_ge(s_ctxT[c], 16)
                if c >= 1:
                    pe.wait_ge(s_query, TILES * c)
                for t in range(TILES):
                    tok = CT * c + t * P
                    ins = T.matmul(psA[:, 2 * t * D:2 * (t + 1) * D], ctxT[:, tok:tok + P], E("wkv"), start=True, stop=True)
                ins.then_inc(s_kvP, 1)

            @for_chunks
            def a_kv_next(c):
                if c + 1 < CHUNKS:
                    a_kv(c + 1)

            @for_chunks
            def a_q(c):
                if c == 0:
                    pe.wait_ge(s_early[1], 16)
                pe.wait_ge(s_xnT["A"], c + 1)
                for t in range(TILES):
                    ins = T.matmul(psA[:, CT + t * D:CT + (t + 1) * D], NORM["A"]["xnT"][:, t * P:(t + 1) * P], E("wq"),
                                   start=True, stop=True)
                ins.then_inc(s_queryP, 1)

            @for_chunks
            def a_val(c):
                for t in range(TILES):
                    pe.wait_ge(s_val, TILES * c + t + 1)
                    if t == 0:
                        pe.wait_ge(s_kv, min(c + 2, CHUNKS))
                    T.transpose(psA[:, t * P:(t + 1) * P], val[:, t, :], ident).then_inc(s_valP, 1)

            @for_chunks
            def a_wo(c):
                pe.wait_ge(s_valT, c + 1)
                for t in range(TILES):
                    ins = T.matmul(psA[:, t * D:(t + 1) * D], valT[:, t * P:(t + 1) * P], E("wo"), start=True, stop=True)
                ins.then_inc(s_woP, 1)

            @for_chunks
            def b_logits(c):
                pe.wait_ge(s_xnT["B"], c + 1)
                for t in range(TILES):
                    ins = T.matmul(psB[:, t * EXPERTS:(t + 1) * EXPERTS], NORM["B"]["xnT"][:, t * P:(t + 1) * P],
                                   E("router"), start=True, stop=True)
                ins.then_inc(s_logit, 1)

            @for_chunks
            def b_comb(c):
                pe.wait_ge(s_parts, c + 1)
                for t in range(TILES):
                    ins = T.transpose(combP[:, t * P:(t + 1) * P],
                                      r_parts[:, t, :, :].rearrange("p a e -> p (a e)"), identb[:])
                ins.then_inc(s_combP, 1)

            @for_chunks
            def b_gate_up(k, c):
                n = STEPS * c + k
                if n == 0:
                    pe.wait_ge(s_smallB, 64)
                    pe.wait_ge(s_wgate, 16)
                    pe.wait_ge(s_wup, 16)
                    pe.wait_ge(s_wdown, 16)
                for w, ps, done, used in ((w_gate, psG, s_gP, s_silu), (w_up, psU, s_uP, s_glu)):
                    pe.wait_ge(s_xnT["B"], c + 1)
                    if n >= 1:
                        pe.wait_ge(used, n)
                    for q in range(2):
                        pair = 2 * k + q
                        ins = T.matmul(ps[:, q * CT:(q + 1) * CT], w[:, pair * P:(pair + 1) * P],
                                       NORM["B"]["xnT"][:], start=True, stop=True)
                    ins.then_inc(done, 1)

            @for_chunks
            def b_spread(k, c):
                n = STEPS * c + k
                if n >= 1:
                    pe.wait_ge(s_hid, n)
                pe.wait_ge(s_combT, c + 1)
                for q in range(2):
                    ins = T.matmul(psC[:, q * CT:(q + 1) * CT], select_s[:, 2 * k + q, :], combT[:], start=True, stop=True)
                ins.then_inc(s_cP, 1)

            @for_chunks
            def b_down(k, c):
                n = STEPS * c + k
                pe.wait_ge(s_hid, n + 1)
                if k == 0 and c >= 1:
                    pe.wait_ge(s_x2, c)
                for q in range(2):
                    for t in range(TILES):
                        first = k == 0 and q == 0 and t == 0
                        last = k == STEPS - 1 and q == 1 and t == TILES - 1
                        ins = T.matmul(psY[:, t * D:(t + 1) * D], hid[:, k % 2, q * CT + t * P:q * CT + (t + 1) * P],
                                       w_down[:, 2 * k + q, :], start=first, stop=last, skip_group_check=True)
                ins.then_inc(s_down, 1)

            @for_chunks
            def c_eo(c):
                if c == 0:
                    pe.wait_ge(s_wff, 1)
                    pe.wait_ge(s_ctxM, 16)
                if c >= 1:
                    pe.wait_ge(s_qT, c)
                T.matmul(psL1[:, CT:2 * CT], L("wx"), ctxT[:, CT * c:CT * (c + 1)], start=True, stop=True).then_inc(s_eoP, 1)

            @for_chunks
            def c_keys(c):
                pe.wait_ge(s_eoT, c + 1)
                T.matmul(psL1[:, 0:CT], L("wx_t"), eoT[:], start=True, stop=True).then_inc(s_keysP, 1)

            @for_chunks
            def c_align(c):
                pe.wait_ge(s_xnT["C"], c + 1)
                pe.wait_ge(s_keysT, c + 1)
                if c >= 1:
                    pe.wait_ge(s_x4, c)
                for t in range(TILES):
                    for rows_of, keys in ((None, eoT), (NORM["C"]["xnT"], keysT)):
                        for s in range(2):
                            at = t * P + s * SEQ
                            lhsT = L("bx_rows") if rows_of is None else rows_of[:, at:at + SEQ]
                            ins = T.matmul(psL0[s * SEQ:(s + 1) * SEQ, t * SEQ:(t + 1) * SEQ], lhsT, keys[:, at:at + SEQ],
                                           start=rows_of is None, stop=rows_of is not None)
                ins.then_inc(s_align, 1)

            @for_chunks
            def c_pT(c):
                pe.wait_ge(s_probs, TILES * (c + 1))
                for t in range(TILES):
                    ins = T.transpose(psL1[0:SEQ, t * P:(t + 1) * P], probs[:, t, :], ident)
                ins.then_inc(s_probsP, 1)

            @for_chunks
            def c_av(c):
                pe.wait_ge(s_probsT, c + 1)
                for t in range(TILES):
                    for s in range(2):
                        at = t * P + s * SEQ
                        ins = T.matmul(psL0[s * SEQ:(s + 1) * SEQ, CT + t * D:CT + (t + 1) * D], probsT[:, at:at + SEQ],
                                       ctxM[:, 2 * (TILES * c + t) + s, :], start=True, stop=True)
                ins.then_inc(s_avP, 1)

            @for_chunks
            def d_weights(c):
                if c == 0:
                    pe.wait_ge(s_late, 32)
                    T.matmul(psL1[:], w_low[:, FF:], w_low[:, 0:FF], start=True, stop=True).then_inc(s_wffP, 1)

            @for_chunks
            def d_ff(c):
                pe.wait_ge(s_xnT["D"], c + 1)
                pe.wait_ge(s_x3, c + 1)
                for f in range(FF_CHUNKS):
                    ps = psL1 if f < 2 else psL0
                    T.matmul(ps[:, (f % 2) * CT:(f % 2 + 1) * CT], w_ff[:, f * P:(f + 1) * P], NORM["D"]["xnT"][:],
                             start=True, stop=True).then_inc(s_ffP, 1)

            @for_chunks
            def d_q(c):
                pe.wait_ge(s_ff, FF_CHUNKS * (c + 1))
                for f in range(FF_CHUNKS):
                    ins = T.matmul(psL1[f * RANK:(f + 1) * RANK, 0:CT], L("u2")[:, f * RANK:(f + 1) * RANK], ff[:, f, :],
                                   start=True, stop=True)
                ins.then_inc(s_qP, 1)

            @for_chunks
            def d_v2(c):
                pe.wait_ge(s_qT, c + 1)
                for t in range(TILES):
                    ins = T.matmul(psL0[:, t * D:(t + 1) * D], qT[:, t * P:(t + 1) * P], L("v2"), start=True, stop=True)
                ins.then_inc(s_ffoutP, 1)

            def warm(ps):
                T.matmul(ps[:, CT:2 * CT], zeros[:, 0:P], zeros[:], start=True, stop=True)

            @for_chunks
            def warm_first(c):
                if c == 0:
                    warm(psL0)

            @for_chunks
            def warm_last(c):
                if c == CHUNKS - 1:
                    warm(psG)

            pe.wait_ge(s_zero, 1)
            for _ in range(2):
                warm(psL0)
            pe.wait_ge(s_early[0], 16)
            a_kv(0)
            for slot in range(SLOTS):
                c0, c1, c2, c3 = slot, slot - 1, slot - 2, slot - 3
                xn_transpose("A", c0)
                b_spread(2, c2)
                b_down(1, c2)
                warm_last(c3)
                a_q(c0)
                b_gate_up(3, c2)
                xn_transpose("B", c1)
                b_down(2, c2)
                d_weights(c0)
                b_logits(c1)
                b_spread(3, c2)
                warm_last(c3)
                a_kv_next(c0)
                xn_transpose("D", c3)
                warm_last(c3)
                d_ff(c3)
                b_down(3, c2)
                d_q(c3)
                b_gate_up(0, c1)
                c_eo(c2)
                d_v2(c3)
                warm_first(c0)
                c_keys(c2)
                warm_last(c2)
                b_gate_up(1, c1)
                warm_first(c0)
                b_comb(c1)
                xn_transpose("C", c2)
                b_spread(0, c1)
                warm_first(c0)
                warm_last(c2)
                c_align(c2)
                b_gate_up(2, c1)
                a_val(c0)
                c_pT(c2)
                warm_last(c2)
                b_spread(1, c1)
                a_wo(c0)
                warm_first(c0)
                b_down(0, c1)
                c_av(c2)



def kernel(x, ctx_1024, g_xattn, g_ffn, L0_xattn_Wq, L0_xattn_Wk, L0_xattn_Wv, L0_xattn_Wo, L0_ffn_router_weight,
           L0_ffn_router_bias, L0_ffn_w_gate, L0_ffn_w_up, L0_ffn_w_down, L1_xattn_W, L1_xattn_b, L1_ffn_U1,
           L1_ffn_V1, L1_ffn_b1, L1_ffn_U2, L1_ffn_V2, L1_ffn_b2):
    import concourse.bacc as _bacc
    from concourse.bass_utils import run_bass_kernel_spmd as _run

    c = np.ascontiguousarray
    xs = c(x).reshape(TOKENS, D)
    cx = c(ctx_1024).reshape(TOKENS, D)
    heads_in = lambda w: c(w).reshape(HEADS, DK, D).transpose(1, 0, 2).reshape(D, D)
    early = np.concatenate([np.eye(P, dtype=xs.dtype), heads_in(L0_xattn_Wk).T, c(L0_xattn_Wv).T, heads_in(L0_xattn_Wq).T,
                            c(L0_xattn_Wo).T, c(L0_ffn_router_weight).T], axis=1)
    late = np.concatenate([
        c(L1_xattn_W).T, c(L1_xattn_W), np.repeat(c(L1_xattn_b).reshape(D, 1), SEQ, axis=1),
        c(L1_ffn_U2).reshape(FF_CHUNKS, P, RANK).transpose(1, 0, 2).reshape(P, FF_CHUNKS * RANK),
        np.concatenate([c(L1_ffn_V2)] * FF_CHUNKS, axis=0),
        c(L1_xattn_b).reshape(D, 1), c(L1_ffn_b1).reshape(FF_CHUNKS, P).T], axis=1)
    experts_in = np.stack([c(w).transpose(2, 0, 1).reshape(D, EXPERTS * INNER)
                           for w in (L0_ffn_w_gate, L0_ffn_w_up)], axis=1)
    experts_out = c(L0_ffn_w_down).transpose(0, 2, 1).reshape(EXPERTS * INNER, D)
    earlier = np.zeros((P, TILES, GROUPS, GROUPS), np.int32)
    for g in range(GROUPS):
        earlier[:, :, g, :g] = 1
    earlier = earlier.reshape(P, TILES * GROUPS * GROUPS)
    bf16 = mybir.dt.np(BF16)
    select = np.zeros((PARTS * EXPERTS, EXPERT_PAIRS, P), bf16)
    for part in range(PARTS):
        for e in range(EXPERTS):
            select[part * EXPERTS + e, e // 2, (e % 2) * INNER:(e % 2 + 1) * INNER] = 1
    arrays = {
        "x": xs, "ctx_t": c(cx.T), "ctx_m": c(cx.reshape(TOKENS // SEQ, SEQ, D).transpose(1, 0, 2)),
        "gates": np.stack([c(g_xattn), c(g_ffn)]), "early": c(early), "late": c(late),
        "experts_in": c(experts_in), "experts_out": c(experts_out), "v1": np.concatenate([c(L1_ffn_V1), c(L1_ffn_U1).T], axis=1),
        "router_bias": c(L0_ffn_router_bias).reshape(1, EXPERTS), "b2": c(L1_ffn_b2).reshape(1, D),
        "earlier": earlier, "select": select, "ident_bf": np.eye(P).astype(bf16)}
    nc = _bacc.Bacc("TRN2", target_bir_lowering=False, num_devices=1)
    args = {k: nc.dram_tensor(f"in_{k}", a.shape, mybir.dt.from_np(a.dtype), kind="ExternalInput").ap()
            for k, a in arrays.items()}
    y = nc.dram_tensor("out_0", (TOKENS, D), F32, kind="ExternalOutput").ap()
    program(nc, out=y, **args)
    r = _run(nc, [{f"in_{k}": a for k, a in arrays.items()}], core_ids=[0])
    return r.results[0]["out_0"].reshape(16, SEQ, D)
```
